# Optimizing a Trainium2 kernel written in Bass

```python
import numpy as np
import jax
import jax.numpy as jnp

def _softmax(x, axis=-1):
    return jax.nn.softmax(x, axis=axis)

def _gelu(x):
    return jax.nn.gelu(x, approximate=True)

def _silu(x):
    return jax.nn.silu(x)

def _sigmoid(x):
    return jax.nn.sigmoid(x)

def _layernorm(x, axis=-1, eps=1e-05):
    m = jnp.mean(x, axis=axis, keepdims=True)
    v = jnp.var(x, axis=axis, keepdims=True)
    return (x - m) / jnp.sqrt(v + eps)

def _scatter_add(tgt, idx, src, axis=0):
    return tgt.at[idx].add(src)

def _segment_sum(src, seg, n):
    return jax.ops.segment_sum(src, seg, n)
kernel_name = 'mk_decoder_postln_d1_seqx_r8_c83080'

def setup_inputs(seed: int=0):
    np.random.seed(seed)
    _w = jnp.asarray

    def _rec_inputs():
        import jax
        import jax.numpy as jnp
        _rk = jax.random.key(seed)
        x = -0.0002928 + 1 * jax.random.normal(jax.random.fold_in(_rk, 1), (4, 256, 128), jnp.float32)
        _lenS = 256 - jax.random.randint(jax.random.fold_in(_rk, 7), (4,), 0, max(1, 256 // 4) + 1, jnp.int32)
        _lenS2 = 512 - jax.random.randint(jax.random.fold_in(_rk, 8), (4,), 0, max(1, 512 // 4) + 1, jnp.int32)
        _ctx_1024P = jax.random.normal(jax.random.fold_in(_rk, 11), (4, 16, 128), jnp.float32)
        _ctx_1024c = jax.random.dirichlet(jax.random.fold_in(_rk, 511), 0.3 * jnp.ones((16,), jnp.float32), (4, 512))
        _ctx_1024t = jnp.einsum('bsk,bkd->bsd', _ctx_1024c, _ctx_1024P)
        _ctx_1024t = _ctx_1024t * jax.lax.rsqrt(jnp.mean(jnp.square(_ctx_1024t)) + 1e-12) * 0.953939
        ctx_1024 = 0.000227908 + 0.99994 * (_ctx_1024t + 0.3 * jax.random.normal(jax.random.fold_in(_rk, 611), (4, 512, 128), jnp.float32))
        return (x, ctx_1024)
    x, ctx_1024 = _rec_inputs()

    def _L0_attn_setup():
        import jax, jax.numpy as jnp
        import numpy as np
        from math import sqrt
        N_HEAD = 16
        W_SCALE = 0.02

        def _reference_tuple_inner(x, W_dq, W_uq, W_dkv, W_uk, W_uv, W_o):
            B, T, C = x.shape
            nh = N_HEAD
            hs = C // nh
            n_kvl = W_dkv.shape[0]
            k_eff = (W_dq.T @ W_uq.T @ W_uk).reshape(nh, hs, n_kvl)
            v_eff = jnp.transpose((W_uv.T @ W_o.T).reshape(n_kvl, nh, hs), (1, 0, 2))
            c_kv = x @ W_dkv.T
            q = x @ W_dq.T @ W_uq.T
            q = q.reshape(B, T, nh, hs)
            q_lat = jnp.einsum('bqhd,hdl->bhql', q, k_eff)
            attn = jnp.einsum('bhql,bkl->bhqk', q_lat, c_kv) / sqrt(hs)
            causal = jnp.tril(jnp.ones((T, T), dtype=bool))
            attn = jnp.where(causal[None, None], attn, -jnp.inf)
            attn = jax.nn.softmax(attn, axis=-1)
            y_lat = jnp.einsum('bhqk,bkl->bhql', attn, c_kv)
            y = jnp.einsum('bhql,hld->bqhd', y_lat, v_eff).reshape(B, T, C)
            return (y, c_kv)
        key = jax.random.key(seed)
        ks = jax.random.split(key, 7)
        B, T, C = (2, 256, 128)
        QL, KVL = (64, 64)
        return {'x': jax.random.normal(ks[0], (B, T, C), dtype=jnp.float32), 'W_dq': jax.random.normal(ks[1], (QL, C), dtype=jnp.float32) * W_SCALE, 'W_uq': jax.random.normal(ks[2], (C, QL), dtype=jnp.float32) * W_SCALE, 'W_dkv': jax.random.normal(ks[3], (KVL, C), dtype=jnp.float32) * W_SCALE, 'W_uk': jax.random.normal(ks[4], (C, KVL), dtype=jnp.float32) * W_SCALE, 'W_uv': jax.random.normal(ks[5], (C, KVL), dtype=jnp.float32) * W_SCALE, 'W_o': jax.random.normal(ks[6], (C, C), dtype=jnp.float32) * W_SCALE}
    _L0_attn_all = _L0_attn_setup()
    _L0_attn_in = {k: v for k, v in _L0_attn_all.items() if k in ('W_dq', 'W_uq', 'W_dkv', 'W_uk', 'W_uv', 'W_o')}
    del _L0_attn_all

    def _L0_xattn_setup():
        import jax, jax.numpy as jnp
        import numpy as np
        HEADS = 16
        key = jax.random.key(seed)
        ks = jax.random.split(key, 6)
        b, n, m, dim = (2, 256, 64, 128)
        s = dim ** (-0.5)
        return {'x': jax.random.normal(ks[0], (b, n, dim), jnp.float32), 'mem': jax.random.normal(ks[1], (b, m, dim), jnp.float32), 'Wq': jax.random.normal(ks[2], (dim, dim), jnp.float32) * s, 'Wkv': jax.random.normal(ks[3], (dim, 2 * dim), jnp.float32) * s, 'Wout': jax.random.normal(ks[4], (dim, dim), jnp.float32) * s, 'bout': jnp.zeros((dim,), jnp.float32)}
    _L0_xattn_all = _L0_xattn_setup()
    _L0_xattn_in = {k: v for k, v in _L0_xattn_all.items() if k in ('Wq', 'Wkv', 'Wout', 'bout')}
    del _L0_xattn_all

    def _L0_ffn_setup():
        import jax, jax.numpy as jnp
        import numpy as np
        D_MODEL = 128
        M = 64
        INNER = 16
        key = jax.random.key(seed)
        ks = jax.random.split(key, 9)

        def init(k, shape, fan_in):
            bound = 1.0 / np.sqrt(fan_in)
            return jax.random.uniform(k, shape, jnp.float32, -bound, bound)
        x = jax.random.normal(ks[0], (16, 512, D_MODEL), dtype=jnp.float32)
        Win = init(ks[1], (D_MODEL, M), D_MODEL)
        bin_ = init(ks[2], (M,), D_MODEL)
        W1 = init(ks[3], (M, INNER), 1)
        b1 = init(ks[4], (M, INNER), 1)
        W2 = init(ks[5], (M, INNER), INNER)
        b2 = init(ks[6], (M,), INNER)
        Wout = init(ks[7], (M, D_MODEL), M)
        bout = init(ks[8], (D_MODEL,), M)
        return {'x': x, 'Win': Win, 'bin_': bin_, 'W1': W1, 'b1': b1, 'W2': W2, 'b2': b2, 'Wout': Wout, 'bout': bout}
    _L0_ffn_all = _L0_ffn_setup()
    _L0_ffn_in = {k: v for k, v in _L0_ffn_all.items() if k in ('Win', 'bin_', 'W1', 'b1', 'W2', 'b2', 'Wout', 'bout')}
    del _L0_ffn_all
    return {'x': x, 'ctx_1024': ctx_1024, 'L0_attn_W_dq': _L0_attn_in['W_dq'], 'L0_attn_W_uq': _L0_attn_in['W_uq'], 'L0_attn_W_dkv': _L0_attn_in['W_dkv'], 'L0_attn_W_uk': _L0_attn_in['W_uk'], 'L0_attn_W_uv': _L0_attn_in['W_uv'], 'L0_attn_W_o': _L0_attn_in['W_o'], 'L0_xattn_Wq': _L0_xattn_in['Wq'], 'L0_xattn_Wkv': _L0_xattn_in['Wkv'], 'L0_xattn_Wout': _L0_xattn_in['Wout'], 'L0_xattn_bout': _L0_xattn_in['bout'], 'L0_ffn_Win': _L0_ffn_in['Win'], 'L0_ffn_bin_': _L0_ffn_in['bin_'], 'L0_ffn_W1': _L0_ffn_in['W1'], 'L0_ffn_b1': _L0_ffn_in['b1'], 'L0_ffn_W2': _L0_ffn_in['W2'], 'L0_ffn_b2': _L0_ffn_in['b2'], 'L0_ffn_Wout': _L0_ffn_in['Wout'], 'L0_ffn_bout': _L0_ffn_in['bout']}

def reference(x, ctx_1024, L0_attn_W_dq, L0_attn_W_uq, L0_attn_W_dkv, L0_attn_W_uk, L0_attn_W_uv, L0_attn_W_o, L0_xattn_Wq, L0_xattn_Wkv, L0_xattn_Wout, L0_xattn_bout, L0_ffn_Win, L0_ffn_bin_, L0_ffn_W1, L0_ffn_b1, L0_ffn_W2, L0_ffn_b2, L0_ffn_Wout, L0_ffn_bout):
    import jax
    import jax.numpy as jnp

    def _L0_attn_ref(x, W_dq, W_uq, W_dkv, W_uk, W_uv, W_o):
        import jax, jax.numpy as jnp
        import numpy as np
        from math import sqrt
        N_HEAD = 16
        W_SCALE = 0.02

        def _reference_tuple_inner(x, W_dq, W_uq, W_dkv, W_uk, W_uv, W_o):
            B, T, C = x.shape
            nh = N_HEAD
            hs = C // nh
            n_kvl = W_dkv.shape[0]
            k_eff = (W_dq.T @ W_uq.T @ W_uk).reshape(nh, hs, n_kvl)
            v_eff = jnp.transpose((W_uv.T @ W_o.T).reshape(n_kvl, nh, hs), (1, 0, 2))
            c_kv = x @ W_dkv.T
            q = x @ W_dq.T @ W_uq.T
            q = q.reshape(B, T, nh, hs)
            q_lat = jnp.einsum('bqhd,hdl->bhql', q, k_eff)
            attn = jnp.einsum('bhql,bkl->bhqk', q_lat, c_kv) / sqrt(hs)
            causal = jnp.tril(jnp.ones((T, T), dtype=bool))
            attn = jnp.where(causal[None, None], attn, -jnp.inf)
            attn = jax.nn.softmax(attn, axis=-1)
            y_lat = jnp.einsum('bhqk,bkl->bhql', attn, c_kv)
            y = jnp.einsum('bhql,hld->bqhd', y_lat, v_eff).reshape(B, T, C)
            return (y, c_kv)
        return _reference_tuple_inner(x, W_dq, W_uq, W_dkv, W_uk, W_uv, W_o)[0]

    def _L0_xattn_ref(x, mem, Wq, Wkv, Wout, bout):
        import jax, jax.numpy as jnp
        import numpy as np
        HEADS = 16
        b, n, dim = x.shape
        h = HEADS
        d = dim // h
        scale = d ** (-0.5)
        mem_len = mem.shape[1]
        q = x @ Wq
        xc = jnp.concatenate((mem, x), axis=1)
        kv = xc @ Wkv
        k, v = jnp.split(kv, 2, axis=-1)

        def to_heads(t):
            bb, nn, _ = t.shape
            return t.reshape(bb, nn, h, d).transpose(0, 2, 1, 3)
        q, k, v = (to_heads(q), to_heads(k), to_heads(v))
        dots = jnp.einsum('bhid,bhjd->bhij', q, k) * scale
        j = dots.shape[-1]
        i_idx = jnp.arange(n)[:, None]
        j_idx = jnp.arange(j)[None, :]
        mask = j_idx > i_idx + mem_len
        dots = jnp.where(mask[None, None], -jnp.inf, dots)
        attn = jax.nn.softmax(dots, axis=-1)
        out = jnp.einsum('bhij,bhjd->bhid', attn, v)
        out = out.transpose(0, 2, 1, 3).reshape(b, n, dim)
        return out @ Wout + bout

    def _L0_ffn_ref(x, Win, bin_, W1, b1, W2, b2, Wout, bout):
        import jax, jax.numpy as jnp
        import numpy as np
        D_MODEL = 128
        M = 64
        INNER = 16
        s = jnp.einsum('btd,dm->btm', x, Win) + bin_
        h = jax.nn.relu(s[..., None] * W1 + b1)
        g = jnp.einsum('btmh,mh->btm', h, W2) + b2
        out = jnp.einsum('btm,md->btd', g, Wout) + bout
        return out
    x = _layernorm(x + _L0_attn_ref(x, L0_attn_W_dq, L0_attn_W_uq, L0_attn_W_dkv, L0_attn_W_uk, L0_attn_W_uv, L0_attn_W_o), axis=-1)
    x = _layernorm(x + _L0_xattn_ref(x, ctx_1024, L0_xattn_Wq, L0_xattn_Wkv, L0_xattn_Wout, L0_xattn_bout), axis=-1)
    x = _layernorm(x + _L0_ffn_ref(x, L0_ffn_Win, L0_ffn_bin_, L0_ffn_W1, L0_ffn_b1, L0_ffn_W2, L0_ffn_b2, L0_ffn_Wout, L0_ffn_bout), axis=-1)
    return x

_drawn_inputs = setup_inputs


def setup_inputs(seed=0):
    import zlib

    import numpy as np

    out = dict(_drawn_inputs(seed))
    spreads = {'L0_xattn_bout': (0.0, 0.1)}
    factors = {'L0_attn_W_dq': 8.0,
     'L0_attn_W_uq': 8.0,
     'L0_attn_W_dkv': 8.0,
     'L0_attn_W_uk': 8.0,
     'L0_attn_W_uv': 8.0,
     'L0_attn_W_o': 8.0,
     'L0_ffn_bin_': 8.0}
    for name, (base, spread) in spreads.items():
        noise = np.random.default_rng([zlib.crc32(name.encode()), seed]).standard_normal(out[name].shape)
        drawn = base * np.exp(spread * noise) if base else spread * noise
        out[name] = jnp.asarray(drawn.astype(out[name].dtype))
    for name, factor in factors.items():
        out[name] = (out[name] * factor).astype(out[name].dtype)
    return out
```

```python
import concourse.bass as bass
from concourse import mybir
from contextlib import ExitStack

F32 = mybir.dt.float32
F32R = mybir.dt.float32r
BF16 = mybir.dt.bfloat16
ALU = mybir.AluOpType
ACT = mybir.ActivationFunctionType
AX = mybir.AxisListType

B, T, C = 4, 256, 128
MEM = 512
NH, HS = 16, 8
KVL = QL = 64
NG, HG = 4, 4
P = 128
QT = T // P
KEYS2 = MEM + T
SLOTS = 3
STACK = HG * SLOTS * HS
ROWS = STACK + 2
SCALE = float(HS) ** -0.5
EPS = 1e-5
NEG = -3.0e38
BANK = 512
FM, FH = 64, 16
FG = FM * FH // P

UNITS = 2 * B
STEPS = UNITS * NG
LAG = 2
SBANKS, TBANKS = 2, 2
PRING = 5

W64 = {"dq": 0, "uqT": 128, "dkv": 256}
WA = {"uk": 0, "uv": 64, "oT": 128, "ident": 256}
WB = {"q": 0, "k": 128, "v": 256, "out": 384, "in2": 512, "fout": 640, "bin": 768, "w1": 769, "b1": 777,
      "w2": 785, "b2": 793, "place": 794}
WB_COLS = 794 + FG * 32


def kind(t):
    return 1 if t < B * NG else 2


def max_banks(t):
    own = [("own", 0, 4, 0), ("own", 0, 2, 1), ("own", 2, 2, 1)]
    if kind(t) == 1:
        return own
    return [("mem", j, 1, qt) for j in range(HG) for qt in range(QT)] + own


def exp_banks(t):
    nk = (2 if kind(t) == 1 else KEYS2 // P)
    return [(kt, h, 2, 0) for kt in range(nk - 1) for h in (0, 2)] + [(nk - 1, 0, 4, P)]


def key_tiles(t):
    return 2 if kind(t) == 1 else KEYS2 // P


def diagonal(t, kt):
    d = kt - (key_tiles(t) - 2)
    return d if d >= 0 else None


def schedule():
    todo = []
    out = []
    slot = [0]
    count = [0]

    def later(delay, *stage):
        count[0] += 1
        todo.append((slot[0] + delay, count[0], stage))

    def emit(stage):
        out.append(stage)
        what, n = stage[0], stage[1]
        if what == "shift":
            return
        if what == "drain":
            later(2, "norm", n)
        elif what == "norm" and n % NG == NG - 1:
            u = n // NG
            if u < B:
                later(1, "ln1", u)
            else:
                later(3, "yT", u - B)
        elif what == "ln1":
            later(5, "x1T", n)
        elif what == "x1T":
            later(2, "proj", n, "q")
            later(4, "proj", n, "k")
            later(6, "proj", n, "v")
        elif what == "proj" and stage[2] in "qk":
            later(1, "spread", n, stage[2])
            if stage[2] == "k":
                later(6, "stack", n, "k")
        elif what == "yT":
            later(2, "wo", n)
        elif what == "wo":
            later(6, "x2T", n)
        elif what == "x2T":
            later(2, "mlp_in", n)
        elif what == "mlp_in":
            for i in range(FG // 2):
                later(3 + i, "hidden", n, i)
        elif what == "hidden" and stage[2] == FG // 2 - 1:
            later(3, "mlp_mid", n)
        elif what == "mlp_mid":
            later(2, "mlp_out", n)

    def due():
        while True:
            ready = sorted(x for x in todo if x[0] <= slot[0])
            if not ready:
                return
            todo.remove(ready[0])
            emit(ready[0][2])

    scores = [(t, i) for t in range(STEPS) for i in range(len(max_banks(t)))]
    at = 0
    for t in range(LAG):
        for i in range(len(max_banks(t))):
            emit(("max", t, i))
            at += 1
        emit(("shift", t))
    for t in range(STEPS):
        banks = exp_banks(t)
        want = sum(len(max_banks(s)) for s in range(min(t + LAG + 1, STEPS)))
        start = at
        n = max(len(banks), want - start)
        for i in range(n):
            slot[0] += 1
            j0, j1 = len(banks) * i // n, len(banks) * (i + 1) // n
            for j in range(j0, j1):
                emit(("exp", t, j))
                kt = banks[j][0]
                if j == len(banks) - 1 or banks[j + 1][0] != kt:
                    later(1, "pv", t, kt)
                    if kt == key_tiles(t) - 1:
                        later(1, "drain", t)
                        if t % NG == NG - 1 and 2 <= t // NG + 2 < UNITS:
                            u = t // NG + 2
                            if u < B:
                                later(1, "restack", u)
                            else:
                                later(1, "stack", u - B, "q")
            goal = start + (want - start) * (i + 1) // n
            while at < goal:
                s, k = scores[at]
                emit(("max", s, k))
                at += 1
                if k == len(max_banks(s)) - 1:
                    later(2, "shift", s)
            due()
    while todo:
        slot[0] += 1
        due()
    return out


def decoder_layer(nc, x_rows, xT, ctxT, w64, wa, wb, sel, biases, out):
    ctx = ExitStack()
    with ctx:
        def sb(name, shape, dt=F32):
            return ctx.enter_context(nc.sbuf_tensor(name, shape, dt))

        def sem(name):
            return ctx.enter_context(nc.semaphore(name))

        plan = schedule()
        place = {s: i for i, s in enumerate(plan)}

        def before(stage, what):
            return sum(1 for s in plan[:place[stage] + 1] if s[0] == what)

        w64_sb = sb("w64_sb", [QL, 384])
        wa_sb = sb("wa_sb", [P, 384])
        wb_sb = sb("wb_sb", [P, WB_COLS])
        sel_r = sb("sel_r", [P, FG * P], F32R)
        bias_sb = sb("bias_sb", [P, 2 * C])
        w2x = sb("w2x", [P, FG, 32])
        low_rows = sb("low_rows", [P, 1])
        ident_b = sb("ident_b", [P, P], BF16)
        neg = sb("neg", [P, P], BF16)
        negT = sb("negT", [P, HG, P], BF16)
        minus_half = sb("minus_half", [P, QT])
        fold = sb("fold", [P, 4, P])
        w1 = sb("w1", [P, 3, P])
        x_sb = sb("x_sb", [P, B * QT, C])
        xT_sb = sb("xT_sb", [P, B * T])
        ctxT_sb = sb("ctxT_sb", [P, B * MEM])
        split0 = sb("split0", [P, 2, 2, 512], F32R)
        ks1 = sb("ks1", [P, NG, B * T], F32R)
        ks2 = sb("ks2", [P, B, NG, KEYS2], F32R)
        qm = sb("qm", [P, 2, NH, T], F32R)
        v1 = sb("v1", [P, B * QT, NH, HS + 1])
        v2 = sb("v2", [P, B, KEYS2 // P, NH, HS + 1])
        probs = sb("probs", [P, PRING, HG, T])
        pmax = sb("pmax", [P, 2, QT * HG, 2])
        nmax = sb("nmax", [P, 2, QT * HG])
        shift_h = sb("shift_h", [HG, NG, T], F32R)
        shift_l = sb("shift_l", [HG, NG, T], F32R)
        headsT = sb("headsT", [P, 2, T])
        rsum = sb("rsum", [P, 2, QT * HG])
        y = sb("y", [P, 2, QT, C])
        res = sb("res", [P, QT, C])
        stats = sb("stats", [P, QT, 6])
        moments = sb("moments", [P, QT, 2])
        vpe = sb("vpe", [P, QT])
        rstd = sb("rstd", [P, QT])
        x1 = sb("x1", [P, B, QT, C])
        x1b = sb("x1b", [P, B, QT, C])
        x1T = sb("x1T", [P, 2, T])
        split_q, split_k = split0[:, 0, :, 0:T], split0[:, 1, :, 0:T]
        yT, feat, feat_h, midT = (xT_sb[:, i * T:(i + 1) * T] for i in range(4))
        hid = ctxT_sb[:, :].rearrange("p (f t) -> p f t", f=FG)
        sel_f = probs[:, 0, :, :].rearrange("p h t -> p (h t)")
        x2 = sb("x2", [P, QT, C])
        x2b = sb("x2b", [P, QT, C])
        x2T = sb("x2T", [P, T])
        feat_s = sb("feat_s", [P, T], F32R)
        x3 = sb("x3", [P, 2, QT, C])

        scr_q1 = nc.dram_tensor("scr_q1", [2, NG * HG, SLOTS, HS, 512], F32, kind="Internal").ap()
        scr_k1 = nc.dram_tensor("scr_k1", [2, NG * HG, SLOTS, HS, 512], F32, kind="Internal").ap()
        scr_m = nc.dram_tensor("scr_m", [B, NG * HG, SLOTS, HS, MEM], F32, kind="Internal").ap()
        scr_q2 = nc.dram_tensor("scr_q2", [B, NG * HG, SLOTS, HS, T], F32, kind="Internal").ap()
        scr_k2 = nc.dram_tensor("scr_k2", [B, NG * HG, SLOTS, HS, T], F32, kind="Internal").ap()
        K_SLOTS = (0, 0, 1)
        Q_SLOTS = (0, 1, 0)

        psum = ctx.enter_context(nc.psum_tensor("psum", [P, 8 * BANK], F32))

        def bank(n):
            return psum[:, n * BANK:(n + 1) * BANK]

        sbank = [bank(i) for i in range(SBANKS)]
        tbank = [bank(SBANKS + i) for i in range(TBANKS)]
        obank = [bank(SBANKS + TBANKS + i) for i in range(2)]
        mbank = [bank(6), bank(7)]

        w64_in, wa_in, wb_in, sel_in, bias_in = (sem(n) for n in ("w64_in", "wa_in", "wb_in", "sel_in", "bias_in"))
        x_in, xT_in, ctxT_in = sem("x_in"), sem("xT_in"), sem("ctxT_in")
        consts_ready = sem("consts_ready")
        neg_step = sem("neg_step")
        pool_step, vec_step = sem("pool_step"), sem("vec_step")
        vec_consts = sem("vec_consts")
        zeroed = sem("zeroed")
        pro_ready = sem("pro_ready")
        pro_hi = sem("pro_hi")
        pro_done = [sem(f"pro_done{i}") for i in range(8)]
        folded = sem("folded")
        spread0 = sem("spread0")
        q_stacked = [sem("q_stacked0"), sem("q_stacked1")]
        k1_stacked = [sem("k1_stacked0"), sem("k1_stacked1")]
        mem_stacked = [sem(f"mem_stacked{b}") for b in range(B)]
        self_stacked = [sem(f"self_stacked{b}") for b in range(B)]
        scores_ready, max_done, nmax_ready = sem("scores_ready"), sem("max_done"), sem("nmax_ready")
        misc_ready = sem("misc_ready")
        misc_freed = [sem("misc_freed0"), sem("misc_freed1")]
        shift_hi = sem("shift_hi")
        shift_loaded = [sem(f"shift_loaded{g}") for g in range(NG)]
        scoresT_ready, exp_done, causal_done, pv_done = (sem(n) for n in ("scoresT_ready", "exp_done", "causal_done", "pv_done"))
        heads_drained, normed = sem("heads_drained"), sem("normed")
        var_ready, rstd_ready, x1_ready, x1b_ready, x2_ready, x2b_ready, x3_ready = (
            sem(n) for n in ("var_ready", "rstd_ready", "x1_ready", "x1b_ready", "x2_ready", "x2b_ready", "x3_ready"))
        split_hi = sem("split_hi")
        hidden_done = sem("hidden_done")
        spread_q, spread_k = [sem(f"spread_q{b}") for b in range(B)], [sem(f"spread_k{b}") for b in range(B)]
        stored = [sem(f"stored{b}") for b in range(B)]

        misc_users = ("shift", "norm", "x1T", "proj", "yT", "wo", "x2T", "mlp_in", "hidden", "mlp_mid", "mlp_out")
        misc_no = {s: n for n, s in enumerate(s for s in plan if s[0] in misc_users)}
        max_no = {s: n for n, s in enumerate(s for s in plan if s[0] == "max")}
        exp_no = {s: n for n, s in enumerate(s for s in plan if s[0] == "exp")}
        pv_no = {s: n for n, s in enumerate(s for s in plan if s[0] == "pv")}
        ln_no = {s: n for n, s in enumerate(s for s in plan if s[0] in ("ln1", "wo", "mlp_out"))}
        causal_no = {s: n for n, s in enumerate(s for s in plan if s[0] == "pv" and kind(s[1]) == 2 and diagonal(s[1], s[2]) is not None)}
        hi_no = {s: n for n, s in enumerate(s for s in plan if s[0] == "proj" and s[2] in "qk")}

        def last_exp(t, kt):
            return 1 + max(exp_no[("exp", t, j)] for j, bk in enumerate(exp_banks(t)) if bk[0] == kt)

        def misc(s):
            n = misc_no[s]
            return mbank[n % 2], misc_freed[n % 2], n // 2

        fold_chain = ["Wq", "WqT", "VE", "KET", "Wv", "Wk"]
        pro = [("q1", 0), ("k1", 0), ("q1", 1), ("k1", 1)] + [("m", b) for b in range(B)]
        pro += [("v1", i) for i in range(2)] + [("vm", b) for b in range(B)]
        split_jobs = [s for s in pro if s[0] in ("q1", "k1", "m")]
        pro_bank = {s: i % 4 for i, s in enumerate(pro)}
        pro_use = {s: i // 4 for i, s in enumerate(pro)}
        PRO_LAST = [sum(1 for s in pro if pro_bank[s] == i) for i in range(4)]

        block = ctx.enter_context(nc.Block())

        @block.sync
        def _(sp):
            sp.dma_start(w64_sb[:, :], w64).then_inc(w64_in, 16)
            sp.dma_start(xT_sb[:, 0:512], xT[:, 0:512]).then_inc(xT_in, 16)
            sp.dma_start(wa_sb[:, :], wa).then_inc(wa_in, 16)
            sp.dma_start(wb_sb[:, :], wb).then_inc(wb_in, 16)
            sp.dma_start(xT_sb[:, 512:], xT[:, 512:]).then_inc(xT_in, 16)
            sp.dma_start(ctxT_sb[:, :], ctxT).then_inc(ctxT_in, 16)
            sp.dma_start(x_sb[:, :, :], x_rows.rearrange("(n p) c -> p n c", p=P)).then_inc(x_in, 16)
            sp.dma_start(bias_sb[:, :], biases.to_broadcast([P, 2 * C])).then_inc(bias_in, 16)
            sp.dma_start(sel_f, sel).then_inc(sel_in, 16)

            def put(scratch, halves, slots, signal):
                for s, part in enumerate(slots):
                    sp.dma_start(scratch[:, s, :, :], halves[:, part, :].bitcast(F32)).then_inc(signal, 16)

            def take_keys(dst, scratch, signal):
                sp.dma_start(dst.bitcast(F32), scratch.rearrange("(g j) s d t -> (j s d) g t", g=NG)).then_inc(signal, 16)

            def take_queries(u, scratch, t0, signal):
                dst = qm[:, u % 2, :, :].rearrange("p (g j) t -> p g j t", g=NG)
                src = scratch.rearrange("(g j) s d t -> j (s d) g t", g=NG)
                rows = SLOTS * HS
                for j in range(HG):
                    sp.dma_start(dst[j * rows:(j + 1) * rows, :, j, :].bitcast(F32),
                                 src[j, :, :, t0:t0 + T]).then_inc(signal, 16)

            sp.wait_ge(zeroed, 3)
            written = 0
            for n, s in enumerate(split_jobs):
                sp.wait_ge(pro_done[pro_bank[s]], pro_use[s] + 1)
                scratch, slots = {"q1": (scr_q1, Q_SLOTS), "k1": (scr_k1, K_SLOTS), "m": (scr_m, K_SLOTS)}[s[0]]
                put(scratch[s[1]], split0[:, n % 2], slots, spread0)
                written += 16 * SLOTS
                sp.wait_ge(spread0, written)
                if s[0] == "q1":
                    if s[1] == 0:
                        take_queries(0, scr_q1[0], 0, q_stacked[0])
                        take_queries(1, scr_q1[0], T, q_stacked[1])
                elif s[0] == "k1":
                    take_keys(ks1[0:STACK, :, 512 * s[1]:512 * (s[1] + 1)], scr_k1[s[1]], k1_stacked[s[1]])
                else:
                    take_keys(ks2[0:STACK, s[1], :, 0:MEM], scr_m[s[1]], mem_stacked[s[1]])

            for s in plan:
                if s[0] == "shift":
                    t = s[1]
                    g = t % NG
                    _, freed, use = misc(s)
                    sp.wait_ge(shift_hi, t + 1)
                    sp.wait_ge(freed, use + 1)
                    for r, part in enumerate((shift_h, shift_l)):
                        row = qm[STACK + r:STACK + r + 1, (t // NG) % 2, g * HG:(g + 1) * HG, :]
                        sp.dma_start(row.bitcast(F32), part[:, g, :].bitcast(F32)).then_inc(shift_loaded[g], 16)
                elif s[0] == "restack":
                    u = s[1]
                    sp.wait_ge(pv_done, before(s, "pv"))
                    take_queries(u, scr_q1[1], (u - 2) * T, q_stacked[u % 2])
                elif s[0] == "spread":
                    b, what = s[1], s[2]
                    _, freed, use = misc(("proj", b, what))
                    sp.wait_ge(freed, use + 1)
                    if what == "q":
                        put(scr_q2[b], split_q, Q_SLOTS, spread_q[b])
                    else:
                        put(scr_k2[b], split_k, K_SLOTS, spread_k[b])
                elif s[0] == "stack":
                    b, what = s[1], s[2]
                    if what == "q":
                        sp.wait_ge(spread_q[b], 16 * SLOTS)
                        sp.wait_ge(pv_done, 1 + max([n for p, n in pv_no.items() if p[1] // NG == B + b - 2]))
                        take_queries(B + b, scr_q2[b], 0, q_stacked[b % 2])
                    else:
                        sp.wait_ge(spread_k[b], 16 * SLOTS)
                        take_keys(ks2[0:STACK, b, :, MEM:], scr_k2[b], self_stacked[b])
                elif s[0] == "mlp_out":
                    b = s[1]
                    sp.wait_ge(x3_ready, b + 1)
                    sp.dma_start(out[b].rearrange("(n p) c -> p n c", p=P), x3[:, b % 2, :, :]).then_inc(stored[b], 16)
            for b in range(B):
                sp.wait_ge(stored[b], 16)

        @block.gpsimd
        def _(pool):
            nc.gpsimd.memset(ks1[STACK:ROWS, :, :].bitcast(F32), 1.0).then_inc(zeroed, 1)
            nc.gpsimd.memset(ks2[STACK:ROWS, :, :, :].bitcast(F32), 1.0).then_inc(consts_ready, 1)
            pool.wait_ge(consts_ready, 1)
            nc.gpsimd.memset(neg[:, :], 0.0).then_inc(neg_step, 1)
            nc.gpsimd.memset(negT[:, :, :], 0.0).then_inc(neg_step, 1)
            pool.wait_ge(neg_step, 2)
            nc.gpsimd.affine_select(out=negT[:, :, :], in_=negT[:, :, :], compare_op=ALU.is_ge, fill=NEG, base=0,
                                    pattern=[[0, HG], [1, P]], channel_multiplier=-1).then_inc(consts_ready, 1)
            nc.gpsimd.affine_select(out=neg[:, :], in_=neg[:, :], compare_op=ALU.is_ge, fill=NEG, base=0,
                                    pattern=[[-1, P]], channel_multiplier=1).then_inc(consts_ready, 1)
            nc.gpsimd.memset(minus_half[:, :], -0.5).then_inc(consts_ready, 1)
            nc.gpsimd.memset(v1[:, :, :, :], 1.0).then_inc(consts_ready, 1)
            nc.gpsimd.memset(v2[:, :, :, :, :], 1.0).then_inc(consts_ready, 1)
            pool.wait_ge(sel_in, 16)
            nc.gpsimd.tensor_copy(sel_r[:, :], sel_f).then_inc(consts_ready, 1)
            steps = 0
            pool.wait_ge(bias_in, 16)
            for s in plan:
                if s[0] == "pv" and s in causal_no:
                    t, kt = s[1], s[2]
                    d = diagonal(t, kt)
                    pool.wait_ge(exp_done, last_exp(t, kt))
                    tile = probs[:, pv_no[s] % PRING, :, d * P:(d + 1) * P]
                    nc.gpsimd.affine_select(out=tile, in_=tile, compare_op=ALU.is_ge, fill=0.0, base=0,
                                            pattern=[[0, HG], [1, P]], channel_multiplier=-1).then_inc(causal_done, 1)
                elif s in ln_no:
                    n = ln_no[s]
                    pool.wait_ge(var_ready, n + 1)
                    nc.gpsimd.tensor_scalar_add(vpe[:, :], moments[:, :, 1], EPS).then_inc(pool_step, 1)
                    steps += 1
                    pool.wait_ge(pool_step, steps)
                    nc.gpsimd.tensor_tensor(rstd[:, :], vpe[:, :], minus_half[:, :], ALU.pow).then_inc(rstd_ready, 1)
                    b = s[1]
                    if s[0] == "ln1":
                        pool.wait_ge(x1_ready, b + 1)
                        for i in range(QT):
                            last = nc.gpsimd.tensor_add(x1b[:, b, i, :], x1[:, b, i, :], bias_sb[:, 0:C])
                        last.then_inc(x1b_ready, 1)
                    elif s[0] == "wo":
                        pool.wait_ge(x2_ready, b + 1)
                        if b:
                            pool.wait_ge(x3_ready, b)
                        for i in range(QT):
                            last = nc.gpsimd.tensor_add(x2b[:, i, :], x2[:, i, :], bias_sb[:, C:2 * C])
                        last.then_inc(x2b_ready, 1)

        @block.scalar
        def _(act):
            for n, s in enumerate(split_jobs):
                act.wait_ge(pro_ready, pro.index(s) + 1)
                if n >= 2:
                    act.wait_ge(spread0, 16 * SLOTS * (n - 1))
                nc.scalar.activation(split0[:, n % 2, 0, :], bank(pro_bank[s]), ACT.Copy).then_inc(pro_hi, 1)
            for s in pro:
                if s[0] in ("v1", "vm"):
                    i = s[1]
                    act.wait_ge(pro_ready, pro.index(s) + 1)
                    if s == ("v1", 0):
                        act.wait_ge(consts_ready, 6)
                    src = bank(pro_bank[s]).rearrange("p (n h d) -> p n h d", n=4, h=NH)
                    if s[0] == "v1":
                        dst = v1[:, 4 * i:4 * i + 4, :, 0:HS]
                    else:
                        dst = v2[:, i, 0:4, :, 0:HS]
                    for k in range(4):
                        last = nc.scalar.activation(dst[:, k], src[:, k], ACT.Copy)
                    last.then_inc(pro_done[pro_bank[s]], 1)

            for s in plan:
                what = s[0]
                if what == "exp":
                    t, j = s[1], s[2]
                    n = exp_no[s]
                    kt, h, nh, q0 = exp_banks(t)[j]
                    ring = pv_no[("pv", t, kt)]
                    act.wait_ge(scoresT_ready, n + 1)
                    if h == 0 and ring >= PRING:
                        act.wait_ge(pv_done, ring - PRING + 1)
                    nq = T - q0
                    src = tbank[n % TBANKS].rearrange("p (h q) -> p h q", h=nh)
                    nc.scalar.activation(probs[:, ring % PRING, h:h + nh, q0:T], src, ACT.Exp,
                                         scale=SCALE).then_inc(exp_done, 1)
                elif what == "shift":
                    t = s[1]
                    g, u = t % NG, t // NG
                    m, freed, use = misc(s)
                    act.wait_ge(misc_ready, misc_no[s] + 1)
                    if u:
                        act.wait_ge(shift_loaded[g], 32 * u)
                    nc.scalar.activation(shift_h[:, g, :], m[0:HG, 0:T], ACT.Copy).then_inc(shift_hi, 1)
                elif what == "drain":
                    t = s[1]
                    act.wait_ge(pv_done, before(s, "pv"))
                    if t >= 2:
                        act.wait_ge(misc_ready, misc_no[("norm", t - 2)] + 1)
                    nc.scalar.activation(headsT[:, t % 2, :], obank[t % 2][:, 0:T], ACT.Copy).then_inc(heads_drained, 1)
                elif what in ("x1T", "yT", "x2T"):
                    b = s[1]
                    m, freed, use = misc(s)
                    act.wait_ge(misc_ready, misc_no[s] + 1)
                    dst = {"x1T": x1T[:, b % 2, :], "yT": yT, "x2T": x2T[:, :]}[what]
                    nc.scalar.activation(dst, m[:, 0:T], ACT.Copy).then_inc(freed, 1)
                elif what == "proj":
                    b, w = s[1], s[2]
                    m, freed, use = misc(s)
                    act.wait_ge(misc_ready, misc_no[s] + 1)
                    if w == "v":
                        for k in range(QT):
                            last = nc.scalar.activation(v2[:, b, MEM // P + k, :, 0:HS],
                                                        m[:, k * P:(k + 1) * P].rearrange("p (h d) -> p h d", h=NH), ACT.Copy)
                        last.then_inc(freed, 1)
                    else:
                        if b:
                            act.wait_ge((spread_q if w == "q" else spread_k)[b - 1], 16 * SLOTS)
                        dst = (split_q if w == "q" else split_k)[:, 0, :]
                        nc.scalar.activation(dst, m[:, 0:T], ACT.Copy).then_inc(split_hi, 1)
                elif what == "hidden":
                    b, i = s[1], s[2]
                    m, freed, use = misc(s)
                    act.wait_ge(misc_ready, misc_no[s] + 1)
                    if b and i == 0:
                        act.wait_ge(misc_ready, misc_no[("mlp_mid", b - 1)] + 1)
                    for k in range(2):
                        f = 2 * i + k
                        last = nc.scalar.activation(hid[:, f, :], m[:, k * T:(k + 1) * T], ACT.Relu,
                                                    scale=wb_sb[:, WB["w1"] + f:WB["w1"] + f + 1],
                                                    bias=wb_sb[:, WB["b1"] + f:WB["b1"] + f + 1])
                    last.then_inc(freed, 1)

        @block.vector
        def _(dve):
            steps = [0]

            def link(ins):
                steps[0] += 1
                ins.then_inc(vec_step, 1)
                dve.wait_ge(vec_step, steps[0])

            nc.vector.memset(qm[:, 0, :, :].bitcast(F32), 0.0).then_inc(zeroed, 1)
            fold_dst = {"Wq": w1[:, 0, :], "WqT": fold[:, 0, :], "KET": fold[0:KVL, 1, :], "VE": fold[0:KVL, 2, :],
                        "Wv": w1[:, 2, :], "Wk": w1[:, 1, :]}
            for n, name in enumerate(fold_chain):
                dve.wait_ge(folded, n + 1)
                rows = KVL if name in ("KET", "VE") else P
                nc.vector.tensor_copy(fold_dst[name], mbank[n % 2][0:rows, 0:P]).then_inc(pro_done[6 + n % 2], 1)
            nc.vector.memset(qm[:, 1, :, :].bitcast(F32), 0.0).then_inc(zeroed, 1)
            for n, s in enumerate(split_jobs):
                dve.wait_ge(pro_hi, n + 1)
                nc.vector.tensor_sub(split0[:, n % 2, 1, :], bank(pro_bank[s]),
                                     split0[:, n % 2, 0, :].bitcast(F32)).then_inc(pro_done[pro_bank[s]], 1)
                if n == 1:
                    dve.wait_ge(wa_in, 16)
                    nc.vector.tensor_copy(ident_b[:, :], wa_sb[:, WA["ident"]:WA["ident"] + P]).then_inc(vec_consts, 1)
                    dve.wait_ge(wb_in, 16)
                    for f in range(FG):
                        last = nc.vector.tensor_scalar(w2x[:, f, :], wb_sb[:, WB["place"] + 32 * f:WB["place"] + 32 * f + 32],
                                                       wb_sb[:, WB["w2"] + f:WB["w2"] + f + 1], None, ALU.mult)
                    last.then_inc(vec_consts, 1)
                    nc.vector.memset(low_rows[0:FM, :], 0.0)
                    nc.vector.memset(low_rows[FM:P, :], -1.0).then_inc(vec_consts, 1)
                    for i in range(2):
                        last = nc.vector.memset(obank[i][:, 0:T], 0.0)
                    last.then_inc(vec_consts, 1)
            dve.wait_ge(x_in, 16)

            def layer_norm(s, dst):
                n = ln_no[s]
                for i in range(QT):
                    last = nc.vector.bn_stats(stats[:, i, :], res[:, i, :])
                link(last)
                for i in range(QT):
                    last = nc.vector.bn_aggr(moments[:, i, :], stats[:, i, :])
                last.then_inc(var_ready, 1)
                dve.wait_ge(rstd_ready, n + 1)
                for i in range(QT):
                    last = nc.vector.tensor_scalar(dst[:, i, :], res[:, i, :], moments[:, i, 0:1], rstd[:, i:i + 1],
                                                   ALU.subtract, ALU.mult)
                return last

            for s in plan:
                what = s[0]
                if what == "max":
                    t, i = s[1], s[2]
                    n = max_no[s]
                    src, j, nh, qt = max_banks(t)[i]
                    dve.wait_ge(scores_ready, n + 1)
                    part = {"mem": 0, "own": 1}[src]
                    width = BANK // nh
                    tile = sbank[n % SBANKS].rearrange("p (h k) -> p h k", h=nh)
                    col = qt * HG + j
                    if kind(t) == 1:
                        nc.vector.tensor_reduce(nmax[:, t % 2, col:col + nh], tile, axis=AX.X, op=ALU.max,
                                                negate=True).then_inc(max_done, 1)
                    else:
                        nc.vector.tensor_reduce(pmax[:, t % 2, col:col + nh, part], tile, axis=AX.X,
                                                op=ALU.max).then_inc(max_done, 1)
                        if i == len(max_banks(t)) - 1:
                            dve.wait_ge(max_done, n + 1)
                            nc.vector.tensor_reduce(nmax[:, t % 2, :], pmax[:, t % 2, :, :], axis=AX.X, op=ALU.max,
                                                    negate=True).then_inc(nmax_ready, 1)
                elif what == "shift":
                    t = s[1]
                    g = t % NG
                    m, freed, use = misc(s)
                    dve.wait_ge(shift_hi, t + 1)
                    nc.vector.tensor_sub(shift_l[:, g, :], m[0:HG, 0:T], shift_h[:, g, :].bitcast(F32)).then_inc(freed, 1)
                elif what == "norm":
                    t = s[1]
                    g, u = t % NG, t // NG
                    m, freed, use = misc(s)
                    dve.wait_ge(misc_ready, misc_no[s] + 1)
                    o = m[:, 0:QT * P].rearrange("p (n r) -> p n r", r=32)
                    link(nc.vector.reciprocal(rsum[:, t % 2, :], o[:, :, HS]))
                    for i in range(QT):
                        dst = y[:, u % 2, i, g * HG * HS:(g + 1) * HG * HS].rearrange("p (j d) -> p j d", j=HG)
                        last = nc.vector.tensor_tensor(dst, o[:, i * HG:(i + 1) * HG, 0:HS],
                                                       rsum[:, t % 2, i * HG:(i + 1) * HG].unsqueeze(2).to_broadcast([P, HG, HS]), ALU.mult)
                    last.then_inc(freed, 1)
                elif what == "ln1":
                    b = s[1]
                    _, freed, use = misc(("norm", 4 * b + 3))
                    dve.wait_ge(freed, use + 1)
                    link(nc.vector.tensor_add(res[:, :, :], y[:, b % 2, :, :], x_sb[:, QT * b:QT * (b + 1), :]))
                    layer_norm(s, x1[:, b]).then_inc(x1_ready, 1)
                elif what == "proj" and s[2] in "qk":
                    b, w = s[1], s[2]
                    m, freed, use = misc(s)
                    dve.wait_ge(split_hi, hi_no[s] + 1)
                    sp_ = split_q if w == "q" else split_k
                    nc.vector.tensor_sub(sp_[:, 1, :], m[:, 0:T], sp_[:, 0, :].bitcast(F32)).then_inc(freed, 1)
                elif what == "wo":
                    b = s[1]
                    m, freed, use = misc(s)
                    dve.wait_ge(misc_ready, misc_no[s] + 1)
                    dve.wait_ge(x1b_ready, b + 1)
                    nc.vector.tensor_add(res[:, :, :].rearrange("p n c -> p (n c)"), m[:, 0:QT * C],
                                         x1b[:, b, :, :].rearrange("p n c -> p (n c)")).then_inc(freed, 1)
                    dve.wait_ge(freed, use + 1)
                    if b:
                        dve.wait_ge(x2b_ready, b)
                    layer_norm(s, x2).then_inc(x2_ready, 1)
                elif what == "mlp_in":
                    b = s[1]
                    m, freed, use = misc(s)
                    dve.wait_ge(misc_ready, misc_no[s] + 1)
                    nc.vector.tensor_scalar(feat, m[:, 0:T], wb_sb[:, WB["bin"]:WB["bin"] + 1], None,
                                            ALU.add).then_inc(freed, 1)
                    dve.wait_ge(freed, use + 1)
                    link(nc.vector.tensor_copy(feat_h.bitcast(F32R), feat))
                    nc.vector.scalar_tensor_tensor(feat_s[:, :], feat_h, low_rows[:, 0:1], feat,
                                                   ALU.mult, ALU.add).then_inc(hidden_done, 1)
                elif what == "mlp_mid":
                    m, freed, use = misc(s)
                    dve.wait_ge(misc_ready, misc_no[s] + 1)
                    nc.vector.tensor_scalar(midT, m[:, 0:T], wb_sb[:, WB["b2"]:WB["b2"] + 1], None,
                                            ALU.add).then_inc(freed, 1)
                elif what == "mlp_out":
                    b = s[1]
                    m, freed, use = misc(s)
                    dve.wait_ge(misc_ready, misc_no[s] + 1)
                    dve.wait_ge(x2b_ready, b + 1)
                    nc.vector.tensor_add(res[:, :, :].rearrange("p n c -> p (n c)"), m[:, 0:QT * C],
                                         x2b[:, :, :].rearrange("p n c -> p (n c)")).then_inc(freed, 1)
                    dve.wait_ge(freed, use + 1)
                    if b >= 2:
                        dve.wait_ge(stored[b - 2], 16)
                    layer_norm(s, x3[:, b % 2]).then_inc(x3_ready, 1)

        @block.tensor
        def _(pe):
            ident = wa_sb[:, WA["ident"]:WA["ident"] + P]

            def w64c(name):
                return w64_sb[:, W64[name]:W64[name] + P]

            def wbc(name):
                return wb_sb[:, WB[name]:WB[name] + P]

            pe.wait_ge(w64_in, 16)
            pe.wait_ge(wa_in, 16)
            operands = {"Wq": (w64c("dq"), w64c("uqT")), "WqT": (w64c("uqT"), w64c("dq")),
                        "VE": (wa_sb[:, WA["uv"]:WA["uv"] + KVL], wa_sb[:, WA["oT"]:WA["oT"] + P]),
                        "KET": (wa_sb[:, WA["uk"]:WA["uk"] + KVL], fold[:, 0, :]),
                        "Wv": (w64c("dkv"), fold[0:KVL, 2, :]), "Wk": (w64c("dkv"), fold[0:KVL, 1, :])}
            for n, name in enumerate(fold_chain):
                lhs, rhs = operands[name]
                if n >= 2:
                    pe.wait_ge(pro_done[6 + n % 2], n // 2)
                if name == "Wk":
                    pe.wait_ge(pro_done[6 + fold_chain.index("KET") % 2], fold_chain.index("KET") // 2 + 1)
                rows = KVL if name in ("KET", "VE") else P
                nc.tensor.matmul(mbank[n % 2][0:rows, 0:P], lhs, rhs, start=True, stop=True).then_inc(folded, 1)

            for i, s in enumerate(pro):
                name, c = s
                bk = bank(pro_bank[s])
                if pro_use[s]:
                    pe.wait_ge(pro_done[pro_bank[s]], pro_use[s])
                if i == 0:
                    pe.wait_ge(xT_in, 32)
                    for k in range(2):
                        pe.wait_ge(pro_done[6 + k], 3)
                if s == ("m", 0):
                    pe.wait_ge(wb_in, 16)
                    pe.wait_ge(ctxT_in, 16)
                if name in ("q1", "k1"):
                    last = nc.tensor.matmul(bk, w1[:, 0 if name == "q1" else 1, :], xT_sb[:, 512 * c:512 * (c + 1)],
                                            start=True, stop=True)
                elif name == "m":
                    last = nc.tensor.matmul(bk, wbc("k"), ctxT_sb[:, MEM * c:MEM * (c + 1)], start=True, stop=True)
                else:
                    for k in range(4):
                        col = 512 * c + k * P
                        lhs = xT_sb[:, col:col + P] if name == "v1" else ctxT_sb[:, col:col + P]
                        last = nc.tensor.matmul(bk[:, k * P:(k + 1) * P], lhs, w1[:, 2, :] if name == "v1" else wbc("v"),
                                                start=True, stop=True)
                last.then_inc(pro_ready, 1)
            pe.wait_ge(consts_ready, 7)
            pe.wait_ge(vec_consts, 4)
            for i in range(4):
                pe.wait_ge(pro_done[i], PRO_LAST[i])

            def open_misc(s):
                m, freed, use = misc(s)
                if use:
                    pe.wait_ge(freed, use)
                return m

            for s in plan:
                what = s[0]
                if what == "max":
                    t, i = s[1], s[2]
                    n = max_no[s]
                    g, u = t % NG, t // NG
                    b = u % B
                    src, j, nh, qt = max_banks(t)[i]
                    if i == 0 and g == 0:
                        pe.wait_ge(q_stacked[u % 2], 16 * HG * (u // 2 + 1))
                        if u < B:
                            pe.wait_ge(k1_stacked[b // 2], 16)
                        else:
                            pe.wait_ge(mem_stacked[b], 16)
                            pe.wait_ge(self_stacked[b], 16)
                    if n >= SBANKS:
                        pe.wait_ge(max_done, n - SBANKS + 1)
                    sk = sbank[n % SBANKS]
                    width = BANK // nh

                    def lhs(jj):
                        return qm[0:STACK, u % 2, g * HG + jj, qt * P:(qt + 1) * P]

                    if src == "mem":
                        last = nc.tensor.matmul(sk, lhs(j), ks2[0:STACK, b, g, 0:MEM], start=True, stop=True)
                    else:
                        for k in range(nh):
                            o = sk[:, k * width:(k + 1) * width]
                            if u < B:
                                keys = ks1[0:STACK, g, b * T:b * T + width]
                            else:
                                keys = ks2[0:STACK, b, g, MEM:MEM + width]
                            nc.tensor.matmul(o, lhs(j + k), keys, start=True, stop=False)
                            last = nc.tensor.matmul(o[:, width - P:width], ident_b[:, :], neg[:, :], start=False, stop=True)
                    last.then_inc(scores_ready, 1)
                elif what == "shift":
                    t = s[1]
                    m = open_misc(s)
                    if kind(t) == 1:
                        pe.wait_ge(max_done, 1 + max_no[("max", t, len(max_banks(t)) - 1)])
                    else:
                        pe.wait_ge(nmax_ready, t - B * NG + 1)
                    for qt in range(QT):
                        last = nc.tensor.transpose(m[0:HG, qt * P:(qt + 1) * P], nmax[:, t % 2, qt * HG:(qt + 1) * HG], ident)
                    last.then_inc(misc_ready, 1)
                elif what == "exp":
                    t, j = s[1], s[2]
                    n = exp_no[s]
                    g, u = t % NG, t // NG
                    b = u % B
                    kt, h, nh, q0 = exp_banks(t)[j]
                    if j == 0:
                        pe.wait_ge(shift_loaded[g], 32 * (u + 1))
                    if n >= TBANKS:
                        pe.wait_ge(exp_done, n - TBANKS + 1)
                    keys = (ks1[0:ROWS, g, b * T + kt * P:b * T + (kt + 1) * P] if u < B
                            else ks2[0:ROWS, b, g, kt * P:(kt + 1) * P])
                    queries = qm[0:ROWS, u % 2, g * HG + h:g * HG + h + nh, q0:T]
                    if kind(t) == 2 or diagonal(t, kt) is None:
                        nc.tensor.matmul(tbank[n % TBANKS], keys, queries, start=True, stop=True).then_inc(scoresT_ready, 1)
                    else:
                        nc.tensor.matmul(tbank[n % TBANKS], keys, queries, start=True, stop=False)
                        tile = tbank[n % TBANKS].rearrange("p (h q) -> p h q", h=nh)[:, :, 0:P]
                        nc.tensor.matmul(tile, ident_b[:, :], negT[:, 0:nh, :], start=False, stop=True).then_inc(scoresT_ready, 1)
                elif what == "pv":
                    t, kt = s[1], s[2]
                    g, u = t % NG, t // NG
                    b = u % B
                    last_kt = key_tiles(t) - 1
                    pe.wait_ge(exp_done, last_exp(t, kt))
                    if s in causal_no:
                        pe.wait_ge(causal_done, causal_no[s] + 1)
                    if kt == 0 and t >= 2:
                        pe.wait_ge(heads_drained, t - 1)
                    q0 = P if kt == last_kt else 0
                    for j in range(HG):
                        v = (v1[:, b * QT + kt, g * HG + j, :] if u < B else v2[:, b, kt, g * HG + j, :])
                        last = nc.tensor.matmul(obank[t % 2][32 * j:32 * j + HS + 1, q0:T], v,
                                                probs[:, pv_no[s] % PRING, j, q0:T], start=(kt == 0), stop=(kt == last_kt))
                    last.then_inc(pv_done, 1)
                elif what == "norm":
                    t = s[1]
                    m = open_misc(s)
                    pe.wait_ge(heads_drained, t + 1)
                    for qt in range(QT):
                        last = nc.tensor.transpose(m[:, qt * P:(qt + 1) * P], headsT[:, t % 2, qt * P:(qt + 1) * P], ident)
                    last.then_inc(misc_ready, 1)
                elif what in ("x1T", "yT", "x2T"):
                    b = s[1]
                    m = open_misc(s)
                    if what == "x1T":
                        pe.wait_ge(x1_ready, b + 1)
                        src = x1[:, b]
                    elif what == "yT":
                        _, freed, use = misc(("norm", NG * (B + b) + NG - 1))
                        pe.wait_ge(freed, use + 1)
                        src = y[:, (B + b) % 2]
                    else:
                        pe.wait_ge(x2_ready, b + 1)
                        src = x2
                    for i in range(QT):
                        last = nc.tensor.transpose(m[:, i * P:(i + 1) * P], src[:, i, :], ident)
                    last.then_inc(misc_ready, 1)
                elif what == "proj":
                    b, w = s[1], s[2]
                    m = open_misc(s)
                    _, freed, use = misc(("x1T", b))
                    pe.wait_ge(freed, use + 1)
                    if w == "v":
                        for i in range(QT):
                            last = nc.tensor.matmul(m[:, i * P:(i + 1) * P], x1T[:, b % 2, i * P:(i + 1) * P], wbc("v"),
                                                    start=True, stop=True)
                    else:
                        last = nc.tensor.matmul(m[:, 0:T], wbc(w), x1T[:, b % 2, :], start=True, stop=True)
                    last.then_inc(misc_ready, 1)
                elif what == "wo":
                    m = open_misc(s)
                    _, freed, use = misc(("yT", s[1]))
                    pe.wait_ge(freed, use + 1)
                    for i in range(QT):
                        last = nc.tensor.matmul(m[:, i * P:(i + 1) * P], yT[:, i * P:(i + 1) * P], wbc("out"), start=True, stop=True)
                    last.then_inc(misc_ready, 1)
                elif what == "mlp_in":
                    m = open_misc(s)
                    _, freed, use = misc(("x2T", s[1]))
                    pe.wait_ge(freed, use + 1)
                    nc.tensor.matmul(m[:, 0:T], wbc("in2"), x2T[:, :], start=True, stop=True).then_inc(misc_ready, 1)
                elif what == "hidden":
                    b, i = s[1], s[2]
                    m = open_misc(s)
                    pe.wait_ge(hidden_done, b + 1)
                    for k in range(2):
                        f = 2 * i + k
                        last = nc.tensor.matmul(m[:, k * T:(k + 1) * T], sel_r[:, f * P:(f + 1) * P], feat_s[:, :], start=True, stop=True)
                    last.then_inc(misc_ready, 1)
                elif what == "mlp_mid":
                    m = open_misc(s)
                    for i in range(FG // 2):
                        _, freed, use = misc(("hidden", s[1], i))
                        pe.wait_ge(freed, use + 1)
                    for f in range(FG):
                        c = f % 4
                        last = nc.tensor.matmul(m[32 * c:32 * c + 32, 0:T], w2x[:, f, :], hid[:, f, :],
                                                start=(f < 4), stop=(f >= 4))
                    last.then_inc(misc_ready, 1)
                elif what == "mlp_out":
                    m = open_misc(s)
                    _, freed, use = misc(("mlp_mid", s[1]))
                    pe.wait_ge(freed, use + 1)
                    for i in range(QT):
                        last = nc.tensor.matmul(m[:, i * P:(i + 1) * P], midT[:, i * P:(i + 1) * P], wbc("fout"), start=True, stop=True)
                    last.then_inc(misc_ready, 1)


def _placed(a):
    import numpy as np
    o = np.zeros((P,) + a.shape[1:], a.dtype)
    for c in range(4):
        for k in range(2):
            o[32 * c + 8 * k:32 * c + 8 * k + 8] = a[8 * c + 32 * k:8 * c + 32 * k + 8]
    return o


def kernel(**inputs):
    import numpy as np
    import concourse.bacc as bacc
    from concourse.bass_utils import run_bass_kernel_spmd

    a = {k.replace("L0_", ""): np.asarray(v) for k, v in inputs.items()}
    f32 = np.float32
    hidden = np.arange(FM * FH).reshape(FG, P)
    feature = hidden // FH
    sel = (np.arange(P)[:, None, None] % FM == feature[None]).reshape(P, FG * P).astype(f32)
    col = (np.arange(FG)[:, None] // 4) * 8 + (np.arange(P)[None, :] // FH)
    place = (np.arange(32)[None, None, :] == col.T[:, :, None]).reshape(P, FG * 32).astype(f32)

    x, c = a["x"], a["ctx_1024"]
    cols = lambda w: w.reshape(FG, P).T
    arrays = {
        "x_rows": x.reshape(B * T, C),
        "xT": x.reshape(B * T, C).T,
        "ctxT": c.reshape(B * MEM, C).T,
        "w64": np.concatenate([a["attn_W_dq"], a["attn_W_uq"].T, a["attn_W_dkv"]], 1),
        "wa": np.concatenate([a["attn_W_uk"], a["attn_W_uv"], a["attn_W_o"].T, np.eye(P, dtype=f32)], 1),
        "wb": np.concatenate([a["xattn_Wq"], a["xattn_Wkv"], a["xattn_Wout"], a["ffn_Win"], a["ffn_Win"],
                              _placed(a["ffn_Wout"]), np.concatenate([a["ffn_bin_"], a["ffn_bin_"]])[:, None],
                              cols(a["ffn_W1"]), cols(a["ffn_b1"]), cols(a["ffn_W2"]),
                              _placed(a["ffn_b2"][:, None]), place], 1),
        "sel": sel,
        "biases": np.concatenate([a["xattn_bout"], a["ffn_bout"]])[None, :],
    }
    arrays = {k: np.ascontiguousarray(v) for k, v in arrays.items()}
    nc = bacc.Bacc("TRN2", target_bir_lowering=False, num_devices=1)
    args = [nc.dram_tensor(k, v.shape, F32, kind="ExternalInput").ap() for k, v in arrays.items()]
    out = nc.dram_tensor("out", (B, T, C), F32, kind="ExternalOutput").ap()
    decoder_layer(nc, *args, out)
    r = run_bass_kernel_spmd(nc, [arrays], core_ids=[0])
    return r.results[0]["out"]
```

```python
import concourse.bass as bass
from concourse import mybir
from contextlib import ExitStack

F32 = mybir.dt.float32
F32R = mybir.dt.float32r
BF16 = mybir.dt.bfloat16
ALU = mybir.AluOpType
ACT = mybir.ActivationFunctionType
AX = mybir.AxisListType

B, T, C = 4, 256, 128
MEM = 512
NH, HS = 16, 8
KVL = QL = 64
NG, HG = 4, 4
P = 128
QT = T // P
KEYS2 = MEM + T
SLOTS = 3
STACK = HG * SLOTS * HS
ROWS = STACK + 2
SCALE = float(HS) ** -0.5
EPS = 1e-5
NEG = -3.0e38
BANK = 512
FM, FH = 64, 16
FG = FM * FH // P

UNITS = 2 * B
STEPS = UNITS * NG
LAG = 9
PV_DELAY = 3
AHEAD = 6
QBUFS = 3
SBANKS, TBANKS, OBANKS, MBANKS = 3, 2, 1, 2
PRING = 6

W64 = {"dq": 0, "uqT": 128, "dkv": 256}
WA = {"uk": 0, "uv": 64, "oT": 128, "ident": 256}
WB = {"q": 0, "k": 128, "v": 256, "out": 384, "in2": 512, "fout": 640, "bin": 768, "w1": 769, "b1": 777,
      "w2": 785, "b2": 793, "place": 794}
WB_COLS = 794 + FG * 32


def kind(t):
    return 1 if t < B * NG else 2


def max_banks(t):
    own = [("own", 0, 4, 0), ("own", 0, 2, 1), ("own", 2, 2, 1)]
    if kind(t) == 1:
        return own
    return [("mem", j, 1, qt) for j in range(HG) for qt in range(QT)] + own


def exp_banks(t):
    nk = (2 if kind(t) == 1 else KEYS2 // P)
    return [(kt, h, 2, 0) for kt in range(nk - 1) for h in (0, 2)] + [(nk - 1, 0, 4, P)]


def key_tiles(t):
    return 2 if kind(t) == 1 else KEYS2 // P


def diagonal(t, kt):
    d = kt - (key_tiles(t) - 2)
    return d if d >= 0 else None


def schedule():
    todo, out, done = [], [], set()
    slot, count = [0], [0]

    def later(delay, *stage):
        count[0] += 1
        todo.append((slot[0] + delay, count[0], stage))

    def emit(*stage):
        out.append(stage)
        done.add(stage)
        what, n = stage[0], stage[1]
        if what == "shift":
            shifted[n] = slot[0]
        elif what == "drain":
            later(1, "norm", n)
            if n % NG == NG - 1 and n // NG + QBUFS < UNITS:
                later(0, "load_q", n // NG + QBUFS)
            if n % NG == NG - 1 and n >= B * NG and n // NG + 2 < UNITS:
                later(0, "load_mem", n // NG + 2 - B)
                later(0, "load_own", n // NG + 2 - B)
        elif what == "norm" and n % NG == NG - 1:
            u = n // NG
            later(*((1, "ln1", u) if u < B else (2, "yT", u - B)))
        elif what == "ln1":
            later(5, "x1T", n)
        elif what == "x1T":
            later(1, "proj", n, "k")
            later(3, "proj", n, "q")
            later(5, "proj", n, "v")
        elif what == "proj" and stage[2] in "qk":
            later(1, "spread", n, stage[2])
            if stage[2] == "k" and n < 2:
                later(5, "load_own", n)
        elif what == "yT":
            later(2, "wo", n)
        elif what == "wo":
            later(5, "x2T", n)
        elif what == "x2T":
            later(2, "mlp_in", n)
        elif what == "mlp_in":
            for i in range(FG // 2):
                later(3 + i, "hidden", n, i)
        elif what == "hidden" and stage[2] == FG // 2 - 1:
            later(2, "mlp_mid", n)
        elif what == "mlp_mid":
            later(2, "mlp_out", n)

    def due():
        while True:
            ready = sorted(x for x in todo if x[0] <= slot[0])
            if not ready:
                return
            todo.remove(ready[0])
            emit(*ready[0][2])

    def loaded(t):
        u = t // NG
        return (u < QBUFS or ("load_q", u) in done) and (u < B or ("load_own", u - B) in done)

    shifted = {}
    maxima = [(t, i) for t in range(STEPS) for i in range(len(max_banks(t)))]
    exps = [(t, j) for t in range(STEPS) for j in range(len(exp_banks(t)))]
    while maxima or exps:
        slot[0] += 1
        if exps:
            t, j = exps[0]
            if j or (t in shifted and slot[0] >= shifted[t] + LAG):
                exps.pop(0)
                banks = exp_banks(t)
                emit("exp", t, j)
                kt = banks[j][0]
                if j == len(banks) - 1 or banks[j + 1][0] != kt:
                    later(PV_DELAY, "pv", t, kt)
                    if kt == key_tiles(t) - 1:
                        later(PV_DELAY, "drain", t)
        if maxima and loaded(maxima[0][0]) and (not exps or maxima[0][0] <= exps[0][0] + AHEAD):
            t, i = maxima.pop(0)
            emit("max", t, i)
            if i == len(max_banks(t)) - 1:
                later(2, "shift", t)
        due()
    while todo:
        slot[0] += 1
        due()
    return out


def decoder_layer(nc, x_rows, xT, ctxT, w64, wa, wb, sel, biases, out):
    ctx = ExitStack()
    with ctx:
        def sb(name, shape, dt=F32):
            return ctx.enter_context(nc.sbuf_tensor(name, shape, dt))

        def sem(name):
            return ctx.enter_context(nc.semaphore(name))

        plan = schedule()
        place = {s: i for i, s in enumerate(plan)}

        def before(stage, what):
            return sum(1 for s in plan[:place[stage] + 1] if s[0] == what)

        w64_sb = sb("w64_sb", [QL, 384])
        wa_sb = sb("wa_sb", [P, 384])
        wb_sb = sb("wb_sb", [P, WB_COLS])
        sel_r = sb("sel_r", [P, FG * P], F32R)
        bias_sb = sb("bias_sb", [P, 2 * C])
        w2x = sb("w2x", [P, FG, 32])
        low_rows = sb("low_rows", [P, 1])
        ident_b = sb("ident_b", [P, P], BF16)
        neg = sb("neg", [P, P], BF16)
        negT = sb("negT", [P, HG, P], BF16)
        minus_half = sb("minus_half", [P, QT])
        fold = sb("fold", [P, 4, P])
        w1 = sb("w1", [P, 3, P])
        x_sb = sb("x_sb", [P, B * QT, C])
        xT_sb = sb("xT_sb", [P, B * T])
        ctxT_sb = sb("ctxT_sb", [P, B * MEM])
        ks1 = sb("ks1", [P, NG, B * T], F32R)
        ks2 = sb("ks2", [P, 2, NG, KEYS2], F32R)
        qm = sb("qm", [P, QBUFS, NH, T], F32R)
        sel_f = sb("sel_f", [P, FG * P])
        split_q = sb("split_q", [P, 2, T], F32R)
        split_k = sb("split_k", [P, 2, T], F32R)
        v1 = sb("v1", [P, B * QT, NH, HS + 1])
        v2 = sb("v2", [P, B, KEYS2 // P, NH, HS + 1])
        probs = sb("probs", [P, PRING, HG, T])
        pmax = sb("pmax", [P, 2, QT * HG, 2])
        nmax = sb("nmax", [P, 2, QT * HG])
        shift_h = sb("shift_h", [HG, NG, T], F32R)
        shift_l = sb("shift_l", [HG, NG, T], F32R)
        headsT = sb("headsT", [P, 2, T])
        rsum = sb("rsum", [P, 2, QT * HG])
        y = sb("y", [P, 2, QT, C])
        res = sb("res", [P, QT, C])
        stats = sb("stats", [P, QT, 6])
        moments = sb("moments", [P, QT, 2])
        vpe = sb("vpe", [P, QT])
        rstd = sb("rstd", [P, QT])
        x1 = sb("x1", [P, B, QT, C])
        x1b = sb("x1b", [P, B, QT, C])
        x1T = sb("x1T", [P, 2, T])
        yT, feat, feat_h, midT = (xT_sb[:, i * T:(i + 1) * T] for i in range(4))
        hid = ctxT_sb[:, :].rearrange("p (f t) -> p f t", f=FG)
        split0 = [probs[:, n % PRING, :, :].rearrange("p (a h) t -> p a (h t)", a=2) for n in range(8)]
        x2 = sb("x2", [P, QT, C])
        x2b = sb("x2b", [P, QT, C])
        x2T = sb("x2T", [P, T])
        feat_s = sb("feat_s", [P, T], F32R)
        x3 = sb("x3", [P, 2, QT, C])

        scr_q1 = nc.dram_tensor("scr_q1", [2, NG * HG, SLOTS, HS, 512], F32, kind="Internal").ap()
        scr_k1 = nc.dram_tensor("scr_k1", [2, NG * HG, SLOTS, HS, 512], F32, kind="Internal").ap()
        scr_m = nc.dram_tensor("scr_m", [B, NG * HG, SLOTS, HS, MEM], F32, kind="Internal").ap()
        scr_q2 = nc.dram_tensor("scr_q2", [B, NG * HG, SLOTS, HS, T], F32, kind="Internal").ap()
        scr_k2 = nc.dram_tensor("scr_k2", [B, NG * HG, SLOTS, HS, T], F32, kind="Internal").ap()
        K_SLOTS = (0, 0, 1)
        Q_SLOTS = (0, 1, 0)

        psum = ctx.enter_context(nc.psum_tensor("psum", [P, 8 * BANK], F32))

        def bank(n):
            return psum[:, n * BANK:(n + 1) * BANK]

        sbank = [bank(i) for i in range(SBANKS)]
        tbank = [bank(SBANKS + i) for i in range(TBANKS)]
        obank = [bank(SBANKS + TBANKS + i) for i in range(OBANKS)]
        mbank = [bank(SBANKS + TBANKS + OBANKS + i) for i in range(MBANKS)]
        fold_bank = [bank(6), bank(7)]

        w64_in, wa_in, wb_in, sel_in, bias_in = (sem(n) for n in ("w64_in", "wa_in", "wb_in", "sel_in", "bias_in"))
        x_in, xT_in, ctxT_in = sem("x_in"), sem("xT_in"), sem("ctxT_in")
        consts_ready = sem("consts_ready")
        neg_step = sem("neg_step")
        pool_step, vec_step = sem("pool_step"), sem("vec_step")
        vec_consts = sem("vec_consts")
        q_zeroed = [sem(f"q_zeroed{i}") for i in range(QBUFS)]
        pro_ready = sem("pro_ready")
        pro_hi = sem("pro_hi")
        pro_done = [sem(f"pro_done{i}") for i in range(8)]
        folded = sem("folded")
        spread0 = [sem(f"spread0_{n}") for n in range(8)]
        q_stacked = [sem(f"q_stacked{i}") for i in range(UNITS)]
        k1_stacked = [sem("k1_stacked0"), sem("k1_stacked1")]
        mem_stacked = [sem(f"mem_stacked{b}") for b in range(B)]
        self_stacked = [sem(f"self_stacked{b}") for b in range(B)]
        scores_ready, max_done, nmax_ready = sem("scores_ready"), sem("max_done"), sem("nmax_ready")
        misc_ready = sem("misc_ready")
        misc_freed = [sem("misc_freed0"), sem("misc_freed1")]
        shift_hi = sem("shift_hi")
        shift_loaded = [sem(f"shift_loaded{g}") for g in range(NG)]
        scoresT_ready, exp_done, causal_done, pv_done = (sem(n) for n in ("scoresT_ready", "exp_done", "causal_done", "pv_done"))
        heads_drained, normed = sem("heads_drained"), sem("normed")
        var_ready, rstd_ready, x1_ready, x1b_ready, x2_ready, x2b_ready, x3_ready = (
            sem(n) for n in ("var_ready", "rstd_ready", "x1_ready", "x1b_ready", "x2_ready", "x2b_ready", "x3_ready"))
        split_hi = sem("split_hi")
        hidden_done = sem("hidden_done")
        spread_q, spread_k = [sem(f"spread_q{b}") for b in range(B)], [sem(f"spread_k{b}") for b in range(B)]
        stored = [sem(f"stored{b}") for b in range(B)]

        misc_users = ("shift", "norm", "x1T", "proj", "yT", "wo", "x2T", "mlp_in", "hidden", "mlp_mid", "mlp_out")
        misc_no = {s: n for n, s in enumerate(s for s in plan if s[0] in misc_users)}
        max_no = {s: n for n, s in enumerate(s for s in plan if s[0] == "max")}
        exp_no = {s: n for n, s in enumerate(s for s in plan if s[0] == "exp")}
        pv_no = {s: n for n, s in enumerate(s for s in plan if s[0] == "pv")}
        ln_no = {s: n for n, s in enumerate(s for s in plan if s[0] in ("ln1", "wo", "mlp_out"))}
        causal_no = {s: n for n, s in enumerate(s for s in plan if s[0] == "pv" and kind(s[1]) == 2 and diagonal(s[1], s[2]) is not None)}
        hi_no = {s: n for n, s in enumerate(s for s in plan if s[0] == "proj" and s[2] in "qk")}

        def last_exp(t, kt):
            return 1 + max(exp_no[("exp", t, j)] for j, bk in enumerate(exp_banks(t)) if bk[0] == kt)

        def unit_pvs(u):
            return 1 + max(n for p, n in pv_no.items() if p[1] // NG == u)

        def misc(s):
            n = misc_no[s]
            return mbank[n % MBANKS], misc_freed[n % MBANKS], n // MBANKS

        fold_chain = ["Wq", "WqT", "VE", "KET", "Wv", "Wk"]
        pro = [("q1", 0), ("k1", 0), ("v1", 0), ("m", 0), ("q1", 1), ("k1", 1), ("m", 1), ("v1", 1), ("vm", 0),
               ("m", 2), ("vm", 1), ("m", 3), ("vm", 2), ("vm", 3)]
        split_jobs = [s for s in pro if s[0] in ("q1", "k1", "m")]
        pro_bank = {s: i % (SBANKS + TBANKS) for i, s in enumerate(pro)}
        pro_use = {s: i // (SBANKS + TBANKS) for i, s in enumerate(pro)}
        PRO_LAST = [sum(1 for s in pro if pro_bank[s] == i) for i in range(SBANKS + TBANKS)]

        block = ctx.enter_context(nc.Block())

        @block.sync
        def _(sp):
            sp.dma_start(w64_sb[:, :], w64).then_inc(w64_in, 16)
            sp.dma_start(wa_sb[:, :], wa).then_inc(wa_in, 16)
            sp.dma_start(xT_sb[:, :], xT).then_inc(xT_in, 16)

            def put(scratch, halves, slots, signal):
                for s, part in enumerate(slots):
                    sp.dma_start(scratch[:, s, :, :], halves[:, part, :]).then_inc(signal, 16)

            def take_keys(dst, scratch, signal):
                sp.dma_start(dst.bitcast(F32), scratch.rearrange("(g j) s d t -> (j s d) g t", g=NG)).then_inc(signal, 16)

            def take_queries(u, scratch, t0, signal):
                dst = qm[:, u % QBUFS, :, :].rearrange("p (g j) t -> p g j t", g=NG)
                src = scratch.rearrange("(g j) s d t -> j (s d) g t", g=NG)
                rows = SLOTS * HS
                for j in range(HG):
                    sp.dma_start(dst[j * rows:(j + 1) * rows, :, j, :].bitcast(F32),
                                 src[j, :, :, t0:t0 + T]).then_inc(signal, 16)

            def load_prologue(n):
                name, c = split_jobs[n]
                sp.wait_ge(spread0[n], 16 * SLOTS)
                if name == "k1":
                    take_keys(ks1[0:STACK, :, 512 * c:512 * (c + 1)], scr_k1[c], k1_stacked[c])
                elif name == "m":
                    if c < 2:
                        take_keys(ks2[0:STACK, c, :, 0:MEM], scr_m[c], mem_stacked[c])
                else:
                    for u in range(2 * c, min(2 * c + 2, QBUFS)):
                        sp.wait_ge(q_zeroed[u], 1)
                        take_queries(u, scr_q1[c], (u % 2) * T, q_stacked[u])

            for n, s in enumerate(split_jobs):
                sp.wait_ge(pro_done[pro_bank[s]], pro_use[s] + 1)
                scratch, slots = {"q1": (scr_q1, Q_SLOTS), "k1": (scr_k1, K_SLOTS), "m": (scr_m, K_SLOTS)}[s[0]]
                put(scratch[s[1]], split0[n], slots, spread0[n])
                if n >= 1:
                    load_prologue(n - 1)
            load_prologue(len(split_jobs) - 1)

            for s in plan:
                if s[0] == "shift":
                    t = s[1]
                    g = t % NG
                    _, freed, use = misc(s)
                    sp.wait_ge(shift_hi, t + 1)
                    sp.wait_ge(freed, use + 1)
                    for r, part in enumerate((shift_h, shift_l)):
                        row = qm[STACK + r:STACK + r + 1, (t // NG) % QBUFS, g * HG:(g + 1) * HG, :]
                        sp.dma_start(row.bitcast(F32), part[:, g, :].bitcast(F32)).then_inc(shift_loaded[g], 16)
                elif s[0] == "spread":
                    b, what = s[1], s[2]
                    _, freed, use = misc(("proj", b, what))
                    sp.wait_ge(freed, use + 1)
                    if what == "q":
                        put(scr_q2[b], split_q[:, :, :].bitcast(F32), Q_SLOTS, spread_q[b])
                    else:
                        put(scr_k2[b], split_k[:, :, :].bitcast(F32), K_SLOTS, spread_k[b])
                elif s[0] == "load_q":
                    u = s[1]
                    sp.wait_ge(pv_done, unit_pvs(u - QBUFS))
                    if u < B:
                        take_queries(u, scr_q1[u // 2], (u % 2) * T, q_stacked[u])
                    else:
                        sp.wait_ge(spread_q[u - B], 16 * SLOTS)
                        take_queries(u, scr_q2[u - B], 0, q_stacked[u])
                elif s[0] == "load_mem":
                    b = s[1]
                    sp.wait_ge(pv_done, unit_pvs(B + b - 2))
                    take_keys(ks2[0:STACK, b % 2, :, 0:MEM], scr_m[b], mem_stacked[b])
                elif s[0] == "load_own":
                    b = s[1]
                    sp.wait_ge(spread_k[b], 16 * SLOTS)
                    take_keys(ks2[0:STACK, b % 2, :, MEM:], scr_k2[b], self_stacked[b])
                elif s[0] == "mlp_out":
                    b = s[1]
                    sp.wait_ge(x3_ready, b + 1)
                    sp.dma_start(out[b].rearrange("(n p) c -> p n c", p=P), x3[:, b % 2, :, :]).then_inc(stored[b], 16)
            for b in range(B):
                sp.wait_ge(stored[b], 16)

        @block.gpsimd
        def _(pool):
            nc.gpsimd.memset(ks1[STACK:ROWS, :, :].bitcast(F32), 1.0).then_inc(neg_step, 1)
            nc.gpsimd.memset(ks2[STACK:ROWS, :, :, :].bitcast(F32), 1.0).then_inc(consts_ready, 1)
            pool.wait_ge(neg_step, 1)
            pool.wait_ge(consts_ready, 1)
            nc.gpsimd.memset(neg[:, :], 0.0).then_inc(neg_step, 1)
            nc.gpsimd.memset(negT[:, :, :], 0.0).then_inc(neg_step, 1)
            pool.wait_ge(neg_step, 3)
            nc.gpsimd.affine_select(out=negT[:, :, :], in_=negT[:, :, :], compare_op=ALU.is_ge, fill=NEG, base=0,
                                    pattern=[[0, HG], [1, P]], channel_multiplier=-1).then_inc(consts_ready, 1)
            nc.gpsimd.affine_select(out=neg[:, :], in_=neg[:, :], compare_op=ALU.is_ge, fill=NEG, base=0,
                                    pattern=[[-1, P]], channel_multiplier=1).then_inc(consts_ready, 1)
            nc.gpsimd.memset(minus_half[:, :], -0.5).then_inc(consts_ready, 1)
            nc.gpsimd.memset(v1[:, :, :, HS], 1.0).then_inc(consts_ready, 1)
            nc.gpsimd.memset(qm[:, 2, :, :].bitcast(F32), 0.0).then_inc(q_zeroed[2], 1)
            nc.gpsimd.memset(v2[:, :, :, :, HS], 1.0).then_inc(consts_ready, 1)
            pool.wait_ge(sel_in, 16)
            nc.gpsimd.tensor_copy(sel_r[:, :], sel_f[:, :]).then_inc(consts_ready, 1)
            steps = 0
            pool.wait_ge(bias_in, 16)
            for s in plan:
                if s[0] == "pv" and s in causal_no:
                    t, kt = s[1], s[2]
                    d = diagonal(t, kt)
                    pool.wait_ge(exp_done, last_exp(t, kt))
                    tile = probs[:, pv_no[s] % PRING, :, d * P:(d + 1) * P]
                    nc.gpsimd.affine_select(out=tile, in_=tile, compare_op=ALU.is_ge, fill=0.0, base=0,
                                            pattern=[[0, HG], [1, P]], channel_multiplier=-1).then_inc(causal_done, 1)
                elif s in ln_no:
                    n = ln_no[s]
                    pool.wait_ge(var_ready, n + 1)
                    nc.gpsimd.tensor_scalar_add(vpe[:, :], moments[:, :, 1], EPS).then_inc(pool_step, 1)
                    steps += 1
                    pool.wait_ge(pool_step, steps)
                    nc.gpsimd.tensor_tensor(rstd[:, :], vpe[:, :], minus_half[:, :], ALU.pow).then_inc(rstd_ready, 1)
                    b = s[1]
                    if s[0] == "ln1":
                        pool.wait_ge(x1_ready, b + 1)
                        for i in range(QT):
                            last = nc.gpsimd.tensor_add(x1b[:, b, i, :], x1[:, b, i, :], bias_sb[:, 0:C])
                        last.then_inc(x1b_ready, 1)
                    elif s[0] == "wo":
                        pool.wait_ge(x2_ready, b + 1)
                        if b:
                            pool.wait_ge(x3_ready, b)
                        for i in range(QT):
                            last = nc.gpsimd.tensor_add(x2b[:, i, :], x2[:, i, :], bias_sb[:, C:2 * C])
                        last.then_inc(x2b_ready, 1)

        @block.scalar
        def _(act):
            act.dma_start(wb_sb[:, :], wb).then_inc(wb_in, 16)
            act.dma_start(ctxT_sb[:, :], ctxT).then_inc(ctxT_in, 16)
            act.dma_start(x_sb[:, :, :], x_rows.rearrange("(n p) c -> p n c", p=P)).then_inc(x_in, 16)
            act.dma_start(bias_sb[:, :], biases.to_broadcast([P, 2 * C])).then_inc(bias_in, 16)
            act.dma_start(sel_f[:, :], sel).then_inc(sel_in, 16)
            for i, s in enumerate(pro):
                act.wait_ge(pro_ready, i + 1)
                if s[0] in ("v1", "vm"):
                    src = bank(pro_bank[s]).rearrange("p (n h d) -> p n h d", n=4, h=NH)
                    dst = (v1[:, 4 * s[1]:4 * s[1] + 4] if s[0] == "v1" else v2[:, s[1], 0:4])[:, :, :, 0:HS]
                    for k in range(4):
                        last = nc.scalar.activation(dst[:, k], src[:, k], ACT.Copy)
                    last.then_inc(pro_done[pro_bank[s]], 1)
                else:
                    n = split_jobs.index(s)
                    if n >= PRING:
                        act.wait_ge(spread0[n - PRING], 16 * SLOTS)
                    nc.scalar.activation(split0[n][:, 0, :].bitcast(F32R), bank(pro_bank[s]), ACT.Copy).then_inc(pro_hi, 1)

            for s in plan:
                what = s[0]
                if what == "exp":
                    t, j = s[1], s[2]
                    n = exp_no[s]
                    kt, h, nh, q0 = exp_banks(t)[j]
                    ring = pv_no[("pv", t, kt)]
                    act.wait_ge(scoresT_ready, n + 1)
                    if h == 0 and ring >= PRING:
                        act.wait_ge(pv_done, ring - PRING + 1)
                    if h == 0 and ring < PRING:
                        for m in range(ring, len(split_jobs), PRING):
                            act.wait_ge(spread0[m], 16 * SLOTS)
                    src = tbank[n % TBANKS].rearrange("p (h q) -> p h q", h=nh)
                    nc.scalar.activation(probs[:, ring % PRING, h:h + nh, q0:T], src, ACT.Exp,
                                         scale=SCALE).then_inc(exp_done, 1)
                elif what == "shift":
                    t = s[1]
                    g, u = t % NG, t // NG
                    m, freed, use = misc(s)
                    act.wait_ge(misc_ready, misc_no[s] + 1)
                    if u:
                        act.wait_ge(shift_loaded[g], 32 * u)
                    nc.scalar.activation(shift_h[:, g, :], m[0:HG, 0:T], ACT.Copy).then_inc(shift_hi, 1)
                elif what == "drain":
                    t = s[1]
                    act.wait_ge(pv_done, before(s, "pv"))
                    if t >= 2:
                        act.wait_ge(misc_ready, misc_no[("norm", t - 2)] + 1)
                    nc.scalar.activation(headsT[:, t % 2, :], obank[t % OBANKS][:, 0:T], ACT.Copy).then_inc(heads_drained, 1)
                elif what in ("x1T", "yT", "x2T"):
                    b = s[1]
                    m, freed, use = misc(s)
                    act.wait_ge(misc_ready, misc_no[s] + 1)
                    dst = {"x1T": x1T[:, b % 2, :], "yT": yT, "x2T": x2T[:, :]}[what]
                    nc.scalar.activation(dst, m[:, 0:T], ACT.Copy).then_inc(freed, 1)
                elif what == "proj":
                    b, w = s[1], s[2]
                    m, freed, use = misc(s)
                    act.wait_ge(misc_ready, misc_no[s] + 1)
                    if w == "v":
                        for k in range(QT):
                            last = nc.scalar.activation(v2[:, b, MEM // P + k, :, 0:HS],
                                                        m[:, k * P:(k + 1) * P].rearrange("p (h d) -> p h d", h=NH), ACT.Copy)
                        last.then_inc(freed, 1)
                    else:
                        if b:
                            act.wait_ge((spread_q if w == "q" else spread_k)[b - 1], 16 * SLOTS)
                        dst = (split_q if w == "q" else split_k)[:, 0, :]
                        nc.scalar.activation(dst, m[:, 0:T], ACT.Copy).then_inc(split_hi, 1)
                elif what == "hidden":
                    b, i = s[1], s[2]
                    m, freed, use = misc(s)
                    act.wait_ge(misc_ready, misc_no[s] + 1)
                    if b and i == 0:
                        act.wait_ge(misc_ready, misc_no[("mlp_mid", b - 1)] + 1)
                    for k in range(2):
                        f = 2 * i + k
                        last = nc.scalar.activation(hid[:, f, :], m[:, k * T:(k + 1) * T], ACT.Relu,
                                                    scale=wb_sb[:, WB["w1"] + f:WB["w1"] + f + 1],
                                                    bias=wb_sb[:, WB["b1"] + f:WB["b1"] + f + 1])
                    last.then_inc(freed, 1)

        @block.vector
        def _(dve):
            steps = [0]

            def link(ins):
                steps[0] += 1
                ins.then_inc(vec_step, 1)
                dve.wait_ge(vec_step, steps[0])

            nc.vector.memset(qm[:, 0, :, :].bitcast(F32), 0.0).then_inc(q_zeroed[0], 1)
            fold_dst = {"Wq": w1[:, 0, :], "WqT": fold[:, 0, :], "KET": fold[0:KVL, 1, :], "VE": fold[0:KVL, 2, :],
                        "Wv": w1[:, 2, :], "Wk": w1[:, 1, :]}
            for n, name in enumerate(fold_chain):
                dve.wait_ge(folded, n + 1)
                rows = KVL if name in ("KET", "VE") else P
                nc.vector.tensor_copy(fold_dst[name], fold_bank[n % 2][0:rows, 0:P]).then_inc(pro_done[6 + n % 2], 1)
            nc.vector.memset(qm[:, 1, :, :].bitcast(F32), 0.0).then_inc(q_zeroed[1], 1)
            for n, s in enumerate(split_jobs):
                dve.wait_ge(pro_hi, n + 1)
                nc.vector.tensor_sub(split0[n][:, 1, :].bitcast(F32R), bank(pro_bank[s]),
                                     split0[n][:, 0, :]).then_inc(pro_done[pro_bank[s]], 1)
                if n == 1:
                    dve.wait_ge(wa_in, 16)
                    nc.vector.tensor_copy(ident_b[:, :], wa_sb[:, WA["ident"]:WA["ident"] + P]).then_inc(vec_consts, 1)
                    dve.wait_ge(wb_in, 16)
                    for f in range(FG):
                        last = nc.vector.tensor_scalar(w2x[:, f, :], wb_sb[:, WB["place"] + 32 * f:WB["place"] + 32 * f + 32],
                                                       wb_sb[:, WB["w2"] + f:WB["w2"] + f + 1], None, ALU.mult)
                    last.then_inc(vec_consts, 1)
                    nc.vector.memset(low_rows[0:FM, :], 0.0)
                    nc.vector.memset(low_rows[FM:P, :], -1.0).then_inc(vec_consts, 1)
                    for i in range(OBANKS):
                        last = nc.vector.memset(obank[i][:, 0:T], 0.0)
                    last.then_inc(vec_consts, 1)
            dve.wait_ge(x_in, 16)

            def layer_norm(s, dst):
                n = ln_no[s]
                for i in range(QT):
                    last = nc.vector.bn_stats(stats[:, i, :], res[:, i, :])
                link(last)
                for i in range(QT):
                    last = nc.vector.bn_aggr(moments[:, i, :], stats[:, i, :])
                last.then_inc(var_ready, 1)
                dve.wait_ge(rstd_ready, n + 1)
                for i in range(QT):
                    last = nc.vector.tensor_scalar(dst[:, i, :], res[:, i, :], moments[:, i, 0:1], rstd[:, i:i + 1],
                                                   ALU.subtract, ALU.mult)
                return last

            for s in plan:
                what = s[0]
                if what == "max":
                    t, i = s[1], s[2]
                    n = max_no[s]
                    src, j, nh, qt = max_banks(t)[i]
                    dve.wait_ge(scores_ready, n + 1)
                    part = {"mem": 0, "own": 1}[src]
                    width = BANK // nh
                    tile = sbank[n % SBANKS].rearrange("p (h k) -> p h k", h=nh)
                    col = qt * HG + j
                    if kind(t) == 1:
                        nc.vector.tensor_reduce(nmax[:, t % 2, col:col + nh], tile, axis=AX.X, op=ALU.max,
                                                negate=True).then_inc(max_done, 1)
                    else:
                        nc.vector.tensor_reduce(pmax[:, t % 2, col:col + nh, part], tile, axis=AX.X,
                                                op=ALU.max).then_inc(max_done, 1)
                        if i == len(max_banks(t)) - 1:
                            dve.wait_ge(max_done, n + 1)
                            nc.vector.tensor_reduce(nmax[:, t % 2, :], pmax[:, t % 2, :, :], axis=AX.X, op=ALU.max,
                                                    negate=True).then_inc(nmax_ready, 1)
                elif what == "shift":
                    t = s[1]
                    g = t % NG
                    m, freed, use = misc(s)
                    dve.wait_ge(shift_hi, t + 1)
                    nc.vector.tensor_sub(shift_l[:, g, :], m[0:HG, 0:T], shift_h[:, g, :].bitcast(F32)).then_inc(freed, 1)
                elif what == "norm":
                    t = s[1]
                    g, u = t % NG, t // NG
                    m, freed, use = misc(s)
                    dve.wait_ge(misc_ready, misc_no[s] + 1)
                    o = m[:, 0:QT * P].rearrange("p (n r) -> p n r", r=32)
                    link(nc.vector.reciprocal(rsum[:, t % 2, :], o[:, :, HS]))
                    for i in range(QT):
                        dst = y[:, u % 2, i, g * HG * HS:(g + 1) * HG * HS].rearrange("p (j d) -> p j d", j=HG)
                        last = nc.vector.tensor_tensor(dst, o[:, i * HG:(i + 1) * HG, 0:HS],
                                                       rsum[:, t % 2, i * HG:(i + 1) * HG].unsqueeze(2).to_broadcast([P, HG, HS]), ALU.mult)
                    last.then_inc(freed, 1)
                elif what == "ln1":
                    b = s[1]
                    _, freed, use = misc(("norm", 4 * b + 3))
                    dve.wait_ge(freed, use + 1)
                    link(nc.vector.tensor_add(res[:, :, :], y[:, b % 2, :, :], x_sb[:, QT * b:QT * (b + 1), :]))
                    layer_norm(s, x1[:, b]).then_inc(x1_ready, 1)
                elif what == "proj" and s[2] in "qk":
                    b, w = s[1], s[2]
                    m, freed, use = misc(s)
                    dve.wait_ge(split_hi, hi_no[s] + 1)
                    sp_ = split_q if w == "q" else split_k
                    nc.vector.tensor_sub(sp_[:, 1, :], m[:, 0:T], sp_[:, 0, :].bitcast(F32)).then_inc(freed, 1)
                elif what == "wo":
                    b = s[1]
                    m, freed, use = misc(s)
                    dve.wait_ge(misc_ready, misc_no[s] + 1)
                    dve.wait_ge(x1b_ready, b + 1)
                    nc.vector.tensor_add(res[:, :, :].rearrange("p n c -> p (n c)"), m[:, 0:QT * C],
                                         x1b[:, b, :, :].rearrange("p n c -> p (n c)")).then_inc(freed, 1)
                    dve.wait_ge(freed, use + 1)
                    if b:
                        dve.wait_ge(x2b_ready, b)
                    layer_norm(s, x2).then_inc(x2_ready, 1)
                elif what == "mlp_in":
                    b = s[1]
                    m, freed, use = misc(s)
                    dve.wait_ge(misc_ready, misc_no[s] + 1)
                    nc.vector.tensor_scalar(feat, m[:, 0:T], wb_sb[:, WB["bin"]:WB["bin"] + 1], None,
                                            ALU.add).then_inc(freed, 1)
                    dve.wait_ge(freed, use + 1)
                    link(nc.vector.tensor_copy(feat_h.bitcast(F32R), feat))
                    nc.vector.scalar_tensor_tensor(feat_s[:, :], feat_h, low_rows[:, 0:1], feat,
                                                   ALU.mult, ALU.add).then_inc(hidden_done, 1)
                elif what == "mlp_mid":
                    m, freed, use = misc(s)
                    dve.wait_ge(misc_ready, misc_no[s] + 1)
                    nc.vector.tensor_scalar(midT, m[:, 0:T], wb_sb[:, WB["b2"]:WB["b2"] + 1], None,
                                            ALU.add).then_inc(freed, 1)
                elif what == "mlp_out":
                    b = s[1]
                    m, freed, use = misc(s)
                    dve.wait_ge(misc_ready, misc_no[s] + 1)
                    dve.wait_ge(x2b_ready, b + 1)
                    nc.vector.tensor_add(res[:, :, :].rearrange("p n c -> p (n c)"), m[:, 0:QT * C],
                                         x2b[:, :, :].rearrange("p n c -> p (n c)")).then_inc(freed, 1)
                    dve.wait_ge(freed, use + 1)
                    if b >= 2:
                        dve.wait_ge(stored[b - 2], 16)
                    layer_norm(s, x3[:, b % 2]).then_inc(x3_ready, 1)

        @block.tensor
        def _(pe):
            ident = wa_sb[:, WA["ident"]:WA["ident"] + P]

            def w64c(name):
                return w64_sb[:, W64[name]:W64[name] + P]

            def wbc(name):
                return wb_sb[:, WB[name]:WB[name] + P]

            pe.wait_ge(w64_in, 16)
            pe.wait_ge(wa_in, 16)
            operands = {"Wq": (w64c("dq"), w64c("uqT")), "WqT": (w64c("uqT"), w64c("dq")),
                        "VE": (wa_sb[:, WA["uv"]:WA["uv"] + KVL], wa_sb[:, WA["oT"]:WA["oT"] + P]),
                        "KET": (wa_sb[:, WA["uk"]:WA["uk"] + KVL], fold[:, 0, :]),
                        "Wv": (w64c("dkv"), fold[0:KVL, 2, :]), "Wk": (w64c("dkv"), fold[0:KVL, 1, :])}
            for n, name in enumerate(fold_chain):
                lhs, rhs = operands[name]
                if n >= 2:
                    pe.wait_ge(pro_done[6 + n % 2], n // 2)
                if name == "Wk":
                    pe.wait_ge(pro_done[6 + fold_chain.index("KET") % 2], fold_chain.index("KET") // 2 + 1)
                rows = KVL if name in ("KET", "VE") else P
                nc.tensor.matmul(fold_bank[n % 2][0:rows, 0:P], lhs, rhs, start=True, stop=True).then_inc(folded, 1)

            for i, s in enumerate(pro):
                name, c = s
                bk = bank(pro_bank[s])
                if pro_use[s]:
                    pe.wait_ge(pro_done[pro_bank[s]], pro_use[s])
                if i == 0:
                    pe.wait_ge(xT_in, 16)
                    for k in range(2):
                        pe.wait_ge(pro_done[6 + k], 3)
                if s == ("m", 0):
                    pe.wait_ge(wb_in, 16)
                    pe.wait_ge(ctxT_in, 16)
                if name in ("q1", "k1"):
                    last = nc.tensor.matmul(bk, w1[:, 0 if name == "q1" else 1, :], xT_sb[:, 512 * c:512 * (c + 1)],
                                            start=True, stop=True)
                elif name == "m":
                    last = nc.tensor.matmul(bk, wbc("k"), ctxT_sb[:, MEM * c:MEM * (c + 1)], start=True, stop=True)
                else:
                    for k in range(4):
                        col = 512 * c + k * P
                        lhs = xT_sb[:, col:col + P] if name == "v1" else ctxT_sb[:, col:col + P]
                        last = nc.tensor.matmul(bk[:, k * P:(k + 1) * P], lhs, w1[:, 2, :] if name == "v1" else wbc("v"),
                                                start=True, stop=True)
                last.then_inc(pro_ready, 1)
            pe.wait_ge(consts_ready, 7)
            pe.wait_ge(vec_consts, 4)
            for i in range(SBANKS + TBANKS):
                pe.wait_ge(pro_done[i], PRO_LAST[i])

            def open_misc(s):
                m, freed, use = misc(s)
                if use:
                    pe.wait_ge(freed, use)
                return m

            for s in plan:
                what = s[0]
                if what == "max":
                    t, i = s[1], s[2]
                    n = max_no[s]
                    g, u = t % NG, t // NG
                    b = u % B
                    src, j, nh, qt = max_banks(t)[i]
                    if i == 0 and g == 0:
                        pe.wait_ge(q_stacked[u], 16 * HG)
                        if u < B:
                            pe.wait_ge(k1_stacked[b // 2], 16)
                        else:
                            pe.wait_ge(mem_stacked[b], 16)
                            pe.wait_ge(self_stacked[b], 16)
                    if n >= SBANKS:
                        pe.wait_ge(max_done, n - SBANKS + 1)
                    sk = sbank[n % SBANKS]
                    width = BANK // nh

                    def lhs(jj):
                        return qm[0:STACK, u % QBUFS, g * HG + jj, qt * P:(qt + 1) * P]

                    if src == "mem":
                        last = nc.tensor.matmul(sk, lhs(j), ks2[0:STACK, b % 2, g, 0:MEM], start=True, stop=True)
                    else:
                        for k in range(nh):
                            o = sk[:, k * width:(k + 1) * width]
                            if u < B:
                                keys = ks1[0:STACK, g, b * T:b * T + width]
                            else:
                                keys = ks2[0:STACK, b % 2, g, MEM:MEM + width]
                            nc.tensor.matmul(o, lhs(j + k), keys, start=True, stop=False)
                            last = nc.tensor.matmul(o[:, width - P:width], ident_b[:, :], neg[:, :], start=False, stop=True)
                    last.then_inc(scores_ready, 1)
                elif what == "shift":
                    t = s[1]
                    m = open_misc(s)
                    if kind(t) == 1:
                        pe.wait_ge(max_done, 1 + max_no[("max", t, len(max_banks(t)) - 1)])
                    else:
                        pe.wait_ge(nmax_ready, t - B * NG + 1)
                    for qt in range(QT):
                        last = nc.tensor.transpose(m[0:HG, qt * P:(qt + 1) * P], nmax[:, t % 2, qt * HG:(qt + 1) * HG], ident)
                    last.then_inc(misc_ready, 1)
                elif what == "exp":
                    t, j = s[1], s[2]
                    n = exp_no[s]
                    g, u = t % NG, t // NG
                    b = u % B
                    kt, h, nh, q0 = exp_banks(t)[j]
                    if j == 0:
                        pe.wait_ge(shift_loaded[g], 32 * (u + 1))
                    if n >= TBANKS:
                        pe.wait_ge(exp_done, n - TBANKS + 1)
                    keys = (ks1[0:ROWS, g, b * T + kt * P:b * T + (kt + 1) * P] if u < B
                            else ks2[0:ROWS, b % 2, g, kt * P:(kt + 1) * P])
                    queries = qm[0:ROWS, u % QBUFS, g * HG + h:g * HG + h + nh, q0:T]
                    if kind(t) == 2 or diagonal(t, kt) is None:
                        nc.tensor.matmul(tbank[n % TBANKS], keys, queries, start=True, stop=True).then_inc(scoresT_ready, 1)
                    else:
                        nc.tensor.matmul(tbank[n % TBANKS], keys, queries, start=True, stop=False)
                        tile = tbank[n % TBANKS].rearrange("p (h q) -> p h q", h=nh)[:, :, 0:P]
                        nc.tensor.matmul(tile, ident_b[:, :], negT[:, 0:nh, :], start=False, stop=True).then_inc(scoresT_ready, 1)
                elif what == "pv":
                    t, kt = s[1], s[2]
                    g, u = t % NG, t // NG
                    b = u % B
                    last_kt = key_tiles(t) - 1
                    pe.wait_ge(exp_done, last_exp(t, kt))
                    if s in causal_no:
                        pe.wait_ge(causal_done, causal_no[s] + 1)
                    if kt == 0 and t >= OBANKS:
                        pe.wait_ge(heads_drained, t - OBANKS + 1)
                    q0 = P if kt == last_kt else 0
                    for j in range(HG):
                        v = (v1[:, b * QT + kt, g * HG + j, :] if u < B else v2[:, b, kt, g * HG + j, :])
                        last = nc.tensor.matmul(obank[t % OBANKS][32 * j:32 * j + HS + 1, q0:T], v,
                                                probs[:, pv_no[s] % PRING, j, q0:T], start=(kt == 0), stop=(kt == last_kt))
                    last.then_inc(pv_done, 1)
                elif what == "norm":
                    t = s[1]
                    m = open_misc(s)
                    pe.wait_ge(heads_drained, t + 1)
                    for qt in range(QT):
                        last = nc.tensor.transpose(m[:, qt * P:(qt + 1) * P], headsT[:, t % 2, qt * P:(qt + 1) * P], ident)
                    last.then_inc(misc_ready, 1)
                elif what in ("x1T", "yT", "x2T"):
                    b = s[1]
                    m = open_misc(s)
                    if what == "x1T":
                        pe.wait_ge(x1_ready, b + 1)
                        src = x1[:, b]
                    elif what == "yT":
                        _, freed, use = misc(("norm", NG * (B + b) + NG - 1))
                        pe.wait_ge(freed, use + 1)
                        src = y[:, (B + b) % 2]
                    else:
                        pe.wait_ge(x2_ready, b + 1)
                        src = x2
                    for i in range(QT):
                        last = nc.tensor.transpose(m[:, i * P:(i + 1) * P], src[:, i, :], ident)
                    last.then_inc(misc_ready, 1)
                elif what == "proj":
                    b, w = s[1], s[2]
                    m = open_misc(s)
                    _, freed, use = misc(("x1T", b))
                    pe.wait_ge(freed, use + 1)
                    if w == "v":
                        for i in range(QT):
                            last = nc.tensor.matmul(m[:, i * P:(i + 1) * P], x1T[:, b % 2, i * P:(i + 1) * P], wbc("v"),
                                                    start=True, stop=True)
                    else:
                        last = nc.tensor.matmul(m[:, 0:T], wbc(w), x1T[:, b % 2, :], start=True, stop=True)
                    last.then_inc(misc_ready, 1)
                elif what == "wo":
                    m = open_misc(s)
                    _, freed, use = misc(("yT", s[1]))
                    pe.wait_ge(freed, use + 1)
                    for i in range(QT):
                        last = nc.tensor.matmul(m[:, i * P:(i + 1) * P], yT[:, i * P:(i + 1) * P], wbc("out"), start=True, stop=True)
                    last.then_inc(misc_ready, 1)
                elif what == "mlp_in":
                    m = open_misc(s)
                    _, freed, use = misc(("x2T", s[1]))
                    pe.wait_ge(freed, use + 1)
                    nc.tensor.matmul(m[:, 0:T], wbc("in2"), x2T[:, :], start=True, stop=True).then_inc(misc_ready, 1)
                elif what == "hidden":
                    b, i = s[1], s[2]
                    m = open_misc(s)
                    pe.wait_ge(hidden_done, b + 1)
                    for k in range(2):
                        f = 2 * i + k
                        last = nc.tensor.matmul(m[:, k * T:(k + 1) * T], sel_r[:, f * P:(f + 1) * P], feat_s[:, :], start=True, stop=True)
                    last.then_inc(misc_ready, 1)
                elif what == "mlp_mid":
                    m = open_misc(s)
                    for i in range(FG // 2):
                        _, freed, use = misc(("hidden", s[1], i))
                        pe.wait_ge(freed, use + 1)
                    for f in range(FG):
                        c = f % 4
                        last = nc.tensor.matmul(m[32 * c:32 * c + 32, 0:T], w2x[:, f, :], hid[:, f, :],
                                                start=(f < 4), stop=(f >= 4))
                    last.then_inc(misc_ready, 1)
                elif what == "mlp_out":
                    m = open_misc(s)
                    _, freed, use = misc(("mlp_mid", s[1]))
                    pe.wait_ge(freed, use + 1)
                    for i in range(QT):
                        last = nc.tensor.matmul(m[:, i * P:(i + 1) * P], midT[:, i * P:(i + 1) * P], wbc("fout"), start=True, stop=True)
                    last.then_inc(misc_ready, 1)


def _placed(a):
    import numpy as np
    o = np.zeros((P,) + a.shape[1:], a.dtype)
    for c in range(4):
        for k in range(2):
            o[32 * c + 8 * k:32 * c + 8 * k + 8] = a[8 * c + 32 * k:8 * c + 32 * k + 8]
    return o


def kernel(**inputs):
    import numpy as np
    import concourse.bacc as bacc
    from concourse.bass_utils import run_bass_kernel_spmd

    a = {k.replace("L0_", ""): np.asarray(v) for k, v in inputs.items()}
    f32 = np.float32
    hidden = np.arange(FM * FH).reshape(FG, P)
    feature = hidden // FH
    sel = (np.arange(P)[:, None, None] % FM == feature[None]).reshape(P, FG * P).astype(f32)
    col = (np.arange(FG)[:, None] // 4) * 8 + (np.arange(P)[None, :] // FH)
    place = (np.arange(32)[None, None, :] == col.T[:, :, None]).reshape(P, FG * 32).astype(f32)

    x, c = a["x"], a["ctx_1024"]
    cols = lambda w: w.reshape(FG, P).T
    arrays = {
        "x_rows": x.reshape(B * T, C),
        "xT": x.reshape(B * T, C).T,
        "ctxT": c.reshape(B * MEM, C).T,
        "w64": np.concatenate([a["attn_W_dq"], a["attn_W_uq"].T, a["attn_W_dkv"]], 1),
        "wa": np.concatenate([a["attn_W_uk"], a["attn_W_uv"], a["attn_W_o"].T, np.eye(P, dtype=f32)], 1),
        "wb": np.concatenate([a["xattn_Wq"], a["xattn_Wkv"], a["xattn_Wout"], a["ffn_Win"], a["ffn_Win"],
                              _placed(a["ffn_Wout"]), np.concatenate([a["ffn_bin_"], a["ffn_bin_"]])[:, None],
                              cols(a["ffn_W1"]), cols(a["ffn_b1"]), cols(a["ffn_W2"]),
                              _placed(a["ffn_b2"][:, None]), place], 1),
        "sel": sel,
        "biases": np.concatenate([a["xattn_bout"], a["ffn_bout"]])[None, :],
    }
    arrays = {k: np.ascontiguousarray(v) for k, v in arrays.items()}
    nc = bacc.Bacc("TRN2", target_bir_lowering=False, num_devices=1)
    args = [nc.dram_tensor(k, v.shape, F32, kind="ExternalInput").ap() for k, v in arrays.items()]
    out = nc.dram_tensor("out", (B, T, C), F32, kind="ExternalOutput").ap()
    decoder_layer(nc, *args, out)
    r = run_bass_kernel_spmd(nc, [arrays], core_ids=[0])
    return r.results[0]["out"]
```

```python
import concourse.bass as bass
from concourse import mybir
from contextlib import ExitStack

F32 = mybir.dt.float32
F32R = mybir.dt.float32r
BF16 = mybir.dt.bfloat16
ALU = mybir.AluOpType
ACT = mybir.ActivationFunctionType
AX = mybir.AxisListType

B, T, C = 4, 256, 128
MEM = 512
NH, HS = 16, 8
KVL = QL = 64
NG, HG = 4, 4
P = 128
QT = T // P
KEYS2 = MEM + T
SLOTS = 3
STACK = HG * SLOTS * HS
ROWS = STACK + 2
PUTS = 2
SCALE = float(HS) ** -0.5
EPS = 1e-5
NEG = -3.0e38
BANK = 512
FM, FH = 64, 16
FG = FM * FH // P

UNITS = 2 * B
STEPS = UNITS * NG
LEAD = 24
AHEAD = 6
PV_LIMIT = 5
QBUFS = 3
SBANKS, TBANKS, OBANKS, MBANKS = 3, 2, 1, 2
PRING = 8

W64 = {"dq": 0, "uqT": 128, "dkv": 256}
WA = {"uk": 0, "uv": 64, "oT": 128, "ident": 256}
WB = {"q": 0, "k": 128, "v": 256, "out": 384, "in2": 512, "fout": 640, "bin": 768, "w1": 769, "b1": 777,
      "w2": 785, "b2": 793, "place": 794}
CHUNKS = [(0, T), (T, T), (2 * T, 2 * T)]
WB_COLS = 794 + FG * 32

PROLOGUE = [("q1", 0), ("k1", 0), ("q1", 1), ("k1", 1), ("v1", 0), ("q1", 2), ("k1", 2), ("m", 0), ("v1", 1), ("vm", 0)]
LATE = [("m", 1), ("vm", 1), ("m", 2), ("vm", 2), ("m", 3), ("vm", 3)]


SPLIT_JOBS = 10
SPLIT_FROM = {7: ("late", "m", 1), 8: ("late", "m", 2), 9: ("late", "m", 3)}
SPLIT_IS = {4: ("q_in", 2), 5: ("k_in", 2), 6: ("m_in", 0), 7: ("m_in", 1), 8: ("scr_m", 2), 9: ("scr_m", 3)}
MISC = ("late", "shift", "norm", "x1T", "proj", "yT", "wo", "x2T", "mlp_in", "hidden", "mlp_mid", "mlp_out")
MLP = ("x2T", "mlp_in", "hidden", "mlp_mid", "mlp_out")
NORMS = ("ln1", "wo", "mlp_out")
MLP_FROM = (28, 28, 28, 26)
MLP_RANKS = (4, 4, 2)
INPUTS_AFTER = 2
COSTS = {"start": 17300, "unit1": 4000, "late_from": 1000, "late_gap": 2500, "latency": 280, "slack": 40,
         "hidden_gap": 500, "keep_act": 6000, "dve_handicap": -1200}
PE_COST = {"max": 210, "exp": 210, "pv": 540, "shift": 214, "norm": 100, "x1T": 427, "yT": 427, "wo": 427, "x2T": 427,
           "proj": 427, "mlp_in": 427, "hidden": 427, "mlp_mid": 960, "mlp_out": 427, "late": 870}
ACT_COST = {"exp": 478, "shift": 264, "drain": 264, "x1T": 264, "yT": 264, "x2T": 264, "proj": 264, "hidden": 902,
            "late": 560}
DVE_COST = {"max": 598, "norm": 100, "proj": 335, "ln1": 1100, "wo": 1100, "mlp_in": 1250, "hidden": 1100,
            "mlp_mid": 392, "mlp_out": 1100, "apply": 512, "late": 600}


def kind(t):
    return 1 if t < B * NG else 2


def max_banks(t):
    own = [("own", 0, 4, 0), ("own", 0, 2, 1), ("own", 2, 2, 1)]
    if kind(t) == 1:
        return own
    return [("mem", j, 1, qt) for j in range(HG) for qt in range(QT)] + own


def exp_banks(t):
    nk = (2 if kind(t) == 1 else KEYS2 // P)
    return [(kt, h, 2, 0) for kt in range(nk - 1) for h in (0, 2)] + [(nk - 1, 0, 4, P)]


def key_tiles(t):
    return 2 if kind(t) == 1 else KEYS2 // P


def diagonal(t, kt):
    d = kt - (key_tiles(t) - 2)
    return d if d >= 0 else None


def schedule():
    out, done = [], {}
    free = {"pe": COSTS["start"], "act": 0, "dve": 0, "pool": 0, "sp": 0}
    chain = []
    misc_freed, max_freed, exp_freed, pv_order = [], [], [], []
    hidden_on_act = set()
    tiles = [0]
    NEVER = float("inf")

    def run(engine, ready, cost):
        free[engine] = max(free[engine], ready + COSTS["latency"]) + cost
        return free[engine]

    def when(*stages):
        return max((done.get(s, NEVER) for s in stages), default=0)

    def loads(t):
        u = t // NG
        if u < B:
            return when(("q_in", u), ("k_in", min(u, 2)))
        return when(("q_in", u), ("m_in", u - B), ("own_in", u - B))

    def ready(s):
        what, n = s[0], s[1]
        if what == "max":
            r = loads(n)
            if s[2] == len(max_banks(n)) - 1 and n >= 2:
                r = max(r, when(("shift", n - 2)) - 1)
            return max(r, max_freed[-SBANKS]) if len(max_freed) >= SBANKS else r
        if what == "exp":
            r = when(("row_in", n))
            place = len(pv_order) + exp_banks(n)[s[2]][0] - sum(1 for x in pv_order if x[1] == n)
            if place >= PRING:
                r = max(r, done[pv_order[place - PRING]] if place - PRING < len(pv_order) else NEVER)
            return max(r, exp_freed[-TBANKS]) if len(exp_freed) >= TBANKS else r
        if what == "pv":
            r = when(("probs", n, s[2]))
            return max(r, when(("drain", n - 1))) if s[2] == 0 and n else r
        r = when(*follows[what](*s[1:]))
        if what == "drain" and n >= 2:
            r = max(r, when(("norm", n - 2)))
        if what in MISC and len(misc_freed) >= MBANKS:
            r = max(r, misc_freed[-MBANKS])
        if what in NORMS and any(x[0] == "apply" for x in chain):
            r = NEVER
        if what == "x2T":
            r = max(r, when(("max", MLP_FROM[n], 0)) - 1)
        if what == "hidden" and n == B - 1:
            r = max(r, when(("mlp_mid", 0)))
        if what == "hidden" and s[2] and n < B - 1:
            r = max(r, when(("hidden", n, s[2] - 1)) + COSTS["hidden_gap"])
        return r

    def emit(s):
        out.append(s)
        what, n = s[0], s[1]
        r = ready(s) if what not in ("max", "exp", "pv") else start(s)
        if s in chain:
            chain.remove(s)
        end = r
        if what in PE_COST:
            cost = PE_COST[what]
            if what == "max":
                cost += {1: 0, 2: 110, 4: 220}[max_banks(n)[s[2]][2]]
            elif what == "exp" and kind(n) == 1:
                cost += 110
            elif what == "pv" and s[2] == key_tiles(n) - 1:
                cost -= 213
            end = run("pe", r - COSTS["latency"], cost)
        if what == "hidden":
            if (max(free["act"], end) + ACT_COST["hidden"] + (COSTS["keep_act"] if exps else 0)
                    <= max(free["dve"], end) + DVE_COST["hidden"]):
                hidden_on_act.add(s)
                end = run("act", end, ACT_COST["hidden"])
            else:
                end = run("dve", end, DVE_COST["hidden"])
        else:
            if what in ACT_COST:
                end = run("act", end, ACT_COST[what])
            if what in DVE_COST and not (what == "proj" and s[2] == "v") and not (what == "late" and s[1] == "vm"):
                end = run("dve", end, DVE_COST[what])
        if what in NORMS:
            end = run("pool", end, 900)
        if what in MISC:
            misc_freed.append(end)
        done[s] = end
        if what == "max":
            max_freed.append(end)
            if s[2] == len(max_banks(n)) - 1:
                done[("nmax", n)] = run("dve", end, 400)
                chain.append(("shift", n))
        elif what == "shift":
            done[("row_in", n)] = run("sp", end, 1250) + 2000
        elif what == "exp":
            exp_freed.append(end)
            banks = exp_banks(n)
            kt = banks[s[2]][0]
            if s[2] == len(banks) - 1 or banks[s[2] + 1][0] != kt:
                if kind(n) == 2 and diagonal(n, kt) is not None:
                    end = run("pool", end, 600)
                done[("probs", n, kt)] = end
                tiles[0] += 1
        elif what == "pv":
            pv_order.append(s)
            if s[2] == key_tiles(n) - 1:
                done[("pvs", n)] = end
                chain.append(("drain", n))
        elif what == "drain":
            chain.append(("norm", n))
            if n % NG == NG - 1:
                u = n // NG
                if u + QBUFS < UNITS:
                    chain.append(("load_q", u + QBUFS))
                if u >= B and u + 2 < UNITS:
                    chain.extend([("load_mem", u + 2 - B), ("load_own", u + 2 - B)])
        elif what == "norm" and n % NG == NG - 1:
            u = n // NG
            chain.append(("ln1", u) if u < B else ("yT", u - B))
        elif what in NORMS:
            chain.append(("apply",) + s)
        elif what == "apply" and n != "mlp_out":
            chain.append(("x1T" if n == "ln1" else "x2T", s[2]))
        elif what == "x1T":
            chain.extend(("proj", n, w) for w in "kqv")
        elif what == "proj" and s[2] in "qk":
            chain.append(("spread", n, s[2]))
            if s[2] == "k" and n < 2:
                chain.append(("load_own", n))
        elif what in ("spread", "load_q", "load_own", "load_mem"):
            done[s] = run("sp", r, 1000 if what != "load_q" else 1800) + 2400
            done[{"spread": s, "load_q": ("q_in", n), "load_own": ("own_in", n), "load_mem": ("m_in", n)}[what]] = done[s]
        elif what in ("yT", "mlp_mid", "x2T"):
            chain.append(({"yT": "wo", "mlp_mid": "mlp_out", "x2T": "mlp_in"}[what], n))
        elif what == "mlp_in":
            chain.extend(("hidden", n, i) for i in range(FG // 2))
        elif what == "hidden" and s[2] == FG // 2 - 1:
            chain.append(("mlp_mid", n))
        elif what == "put0":
            chain.append(("load0", n))
            done[s] = run("pool", r, 1000) + 5000
        elif what == "load0":
            end = run("pool", r, 1000) + 5000
            done[SPLIT_IS[n]] = end

    def start(s):
        return max(ready(s), free["pe"])

    u_last = lambda u: ("norm", u * NG + NG - 1)
    follows = {"shift": lambda t: [("nmax", t)], "drain": lambda t: [("pvs", t)], "norm": lambda t: [("drain", t)],
               "ln1": lambda b: [u_last(b)], "yT": lambda b: [u_last(B + b)], "wo": lambda b: [("yT", b)],
               "apply": lambda what, b: [(what, b)], "x1T": lambda b: [("apply", "ln1", b)],
               "x2T": lambda b: [("apply", "wo", b)], "proj": lambda b, w: [("x1T", b)],
               "spread": lambda b, w: [("proj", b, w)], "mlp_in": lambda b: [("x2T", b)],
               "hidden": lambda b, i: [("mlp_in", b)], "mlp_mid": lambda b: [("hidden", b, FG // 2 - 1)],
               "mlp_out": lambda b: [("mlp_mid", b)],
               "load_q": lambda u: [("drain", (u - QBUFS) * NG + NG - 1)] + ([("spread", u - B, "q")] if u >= B else []),
               "load_own": lambda b: [("spread", b, "k")] + ([("drain", (B + b - 2) * NG + NG - 1)] if b >= 2 else []),
               "load_mem": lambda b: [("drain", (B + b - 2) * NG + NG - 1)],
               "late": lambda name, c: [], "put0": lambda n: [SPLIT_FROM[n]] if n in SPLIT_FROM else [],
               "load0": lambda n: [("put0", n)], "inputs": lambda t: [("shift", t)]}
    for u in range(2):
        done[("q_in", u)] = done[("k_in", u)] = COSTS["start"] + u * COSTS["unit1"]
    done[("m_in", 2)] = done[("m_in", 3)] = NEVER
    chain += [("inputs", INPUTS_AFTER)] + [("late",) + job for job in LATE] + [("put0", n) for n in range(4, SPLIT_JOBS)]
    maxima = [(t, i) for t in range(STEPS) for i in range(len(max_banks(t)))]
    exps = [(t, j) for t in range(STEPS) for j in range(len(exp_banks(t)))]
    pvs = [(t, kt) for t in range(STEPS) for kt in range(0, key_tiles(t), 2)]
    lead = 0
    while maxima or exps or pvs or chain:
        now = free["pe"]
        idle = [s for s in chain if s[0] not in MISC and ready(s) <= now + COSTS["slack"]]
        if idle:
            emit(idle[0])
            continue
        best = [(NEVER, 0, 0, None)]
        for k, s in enumerate(chain):
            if s[0] == "late":
                due = COSTS["start"] + COSTS["late_from"] + COSTS["late_gap"] * LATE.index(s[1:])
                best.append((max(now, ready(s), due), 0, k, s))
            elif s[0] in MISC:
                best.append((max(now, ready(s)), MLP_RANKS[s[1]] if s[0] in MLP and s[1] < B - 1 else 0, k, s))
        if pvs:
            t, kt = pvs[0]
            s = ("pv", t, kt + 1)
            rank = 1 if tiles[0] - len(pv_order) >= PV_LIMIT else 3
            best.append((max(now, ready(("pv", t, kt)), ready(s)), rank, 0, ("pv", t, kt)))
        if exps:
            s = ("exp",) + exps[0]
            best.append((max(now, ready(s)), 2, free["act"], s))
        if maxima and (not exps or (maxima[0][0] <= exps[0][0] + AHEAD and lead < LEAD)):
            s = ("max",) + maxima[0]
            best.append((max(now, ready(s)), 2, free["dve"] + COSTS["dve_handicap"], s))
        soon = [x for x in best if x[0] <= now + COSTS["slack"]]
        pick = (min(soon, key=lambda x: (x[1], x[2])) if soon else min(best, key=lambda x: (x[0], x[1], x[2])))
        if pick[0] == NEVER:
            nxt = [s for s in chain if s[0] not in MISC]
            assert nxt, (best, chain)
            s = min(nxt, key=ready)
            assert ready(s) < NEVER, (best, chain)
            free["pe"] = max(now, ready(s))
            emit(s)
            continue
        waiting = [s for s in chain if s[0] not in MISC and ready(s) < pick[0]]
        if waiting:
            emit(min(waiting, key=ready))
            continue
        s = pick[3]
        if s[0] == "max":
            maxima.pop(0)
            lead += 1
        elif s[0] == "exp":
            exps.pop(0)
            lead -= 1
        elif s[0] == "pv":
            pvs.pop(0)
            emit(s)
            s = ("pv", s[1], s[2] + 1)
        emit(s)
    return out, hidden_on_act


def decoder_layer(nc, x_rows, xT, ctxT, w64, wa, wb, sel, biases, out):
    ctx = ExitStack()
    with ctx:
        def sb(name, shape, dt=F32):
            return ctx.enter_context(nc.sbuf_tensor(name, shape, dt))

        def sem(name):
            return ctx.enter_context(nc.semaphore(name))

        plan, hidden_on_act = schedule()
        place = {s: i for i, s in enumerate(plan)}

        def before(stage, what):
            return sum(1 for s in plan[:place[stage] + 1] if s[0] == what)

        w64_sb = sb("w64_sb", [QL, 384])
        wa_sb = sb("wa_sb", [P, 384])
        wb_sb = sb("wb_sb", [P, WB_COLS])
        sel_r = sb("sel_r", [P, FG * P], F32R)
        bias_sb = sb("bias_sb", [P, 2 * C])
        w2x = sb("w2x", [P, FG, 32])
        low_rows = sb("low_rows", [P, 1])
        ident_b = sb("ident_b", [P, P], BF16)
        neg = sb("neg", [P, HG, P], BF16)
        negT = sb("negT", [P, HG, P], BF16)
        minus_half = sb("minus_half", [P, QT])
        fold = sb("fold", [P, 4, P])
        w1 = sb("w1", [P, 3, P])
        x_sb = sb("x_sb", [P, B * QT, C])
        xT_sb = sb("xT_sb", [P, B * T])
        ctxT_sb = sb("ctxT_sb", [P, B * MEM])
        ks1 = sb("ks1", [P, NG, B * T], F32R)
        ks2 = sb("ks2", [P, 2, NG, KEYS2], F32R)
        qm = sb("qm", [P, QBUFS, NH, T], F32R)
        sel_f = sb("sel_f", [P, FG * P])
        split_q = sb("split_q", [P, 2, T], F32R)
        split_k = sb("split_k", [P, 2, T], F32R)
        v1 = sb("v1", [P, B * QT, NH, HS + 1])
        v2 = sb("v2", [P, B, KEYS2 // P, NH, HS + 1])
        probs = sb("probs", [P, PRING, HG, T])
        pmax = sb("pmax", [P, 2, QT * HG, 2])
        nmax = sb("nmax", [P, 2, QT * HG])
        nmax_s = sb("nmax_s", [P, 2, QT, 2 * HG])
        shift_rows = sb("shift_rows", [2 * HG, 2, T], F32R)
        headsT = sb("headsT", [P, 2, T])
        rsum = sb("rsum", [P, 2, QT * HG])
        y = sb("y", [P, 2, QT, C])
        res = sb("res", [P, QT, C])
        stats = sb("stats", [P, QT, 6])
        moments = sb("moments", [P, QT, 2])
        vpe = sb("vpe", [P, QT])
        rstd = sb("rstd", [P, QT])
        x1 = sb("x1", [P, B, QT, C])
        x1b = sb("x1b", [P, B, QT, C])
        x1T = sb("x1T", [P, 2, T])
        hid_own = sb("hid_own", [P, FG * T])
        yT, feat, feat_h = (xT_sb[:, i * T:(i + 1) * T] for i in range(3))
        old_values = v1.rearrange("p n h d -> p (n h d)")
        x2T = [old_values[:, b * T:(b + 1) * T] for b in range(B)]
        old_fold, old_w1 = fold.rearrange("p n c -> p (n c)"), w1.rearrange("p n c -> p (n c)")
        midT = [xT_sb[:, 3 * T:4 * T], old_fold[:, 0:T], old_fold[:, T:2 * T], old_w1[:, 0:T]]
        old_rows = x_sb.rearrange("p n c -> p (n c)")
        hid_ctx = [ctxT_sb[:, f * T:(f + 1) * T] for f in range(FG)]
        hid = [hid_ctx, [hid_own[:, f * T:(f + 1) * T] for f in range(FG)],
               [x[:, f * T:(f + 1) * T] for x in (old_rows, sel_f) for f in range(FG // 2)], hid_ctx]
        feat_s = [x[:, i, :] for x in (split_q, split_k) for i in range(2)]
        split0 = [probs[:, n, :, :].rearrange("p (a h) t -> p a (h t)", a=2) for n in range(PRING)]
        split0 += [x.rearrange("p b q c -> p (b q c)").rearrange("p (a t) -> p a t", a=2) for x in (x1, x1b)]

        scr_q1 = nc.dram_tensor("scr_q1", [P, SLOTS, B * T], F32, kind="Internal").ap()
        scr_k1 = nc.dram_tensor("scr_k1", [P, SLOTS, B * T], F32, kind="Internal").ap()
        scr_m = nc.dram_tensor("scr_m", [B, P, SLOTS, MEM], F32, kind="Internal").ap()
        scr_q2 = nc.dram_tensor("scr_q2", [B, P, SLOTS, T], F32, kind="Internal").ap()
        scr_k2 = nc.dram_tensor("scr_k2", [B, P, SLOTS, T], F32, kind="Internal").ap()
        Q_SLOTS = (0, 2)
        K_SLOTS = (1, 0)

        psum = ctx.enter_context(nc.psum_tensor("psum", [P, 8 * BANK], F32))

        def bank(n):
            return psum[:, n * BANK:(n + 1) * BANK]

        sbank = [bank(i) for i in range(SBANKS)]
        tbank = [bank(SBANKS + i) for i in range(TBANKS)]
        obank = [bank(SBANKS + TBANKS + i) for i in range(OBANKS)]
        mbank = [bank(SBANKS + TBANKS + OBANKS + i) for i in range(MBANKS)]
        fold_bank = [bank(6), bank(7)]

        w64_in, wa_in, wb_in, sel_in, bias_in = (sem(n) for n in ("w64_in", "wa_in", "wb_in", "sel_in", "bias_in"))
        x_in, xT_in, xT_rest_in, ctxT_in = sem("x_in"), sem("xT_in"), sem("xT_rest_in"), sem("ctxT_in")
        sel_ready = sem("sel_ready")
        consts_ready = sem("consts_ready")
        neg_step = sem("neg_step")
        ones_ready = sem("ones_ready")
        pool_step, vec_step = sem("pool_step"), sem("vec_step")
        vec_consts = sem("vec_consts")
        q_zeroed = [sem(f"q_zeroed{i}") for i in range(QBUFS)]
        pro_ready = sem("pro_ready")
        pro_hi = sem("pro_hi")
        pro_done = [sem(f"pro_done{i}") for i in range(8)]
        folded = sem("folded")
        spread0 = [sem(f"spread0_{n}") for n in range(10)]
        q_stacked = [sem(f"q_stacked{i}") for i in range(UNITS)]
        k1_stacked = [sem(f"k1_stacked{c}") for c in range(len(CHUNKS))]
        mem_stacked = [sem(f"mem_stacked{b}") for b in range(B)]
        self_stacked = [sem(f"self_stacked{b}") for b in range(B)]
        scores_ready, max_done, nmax_ready = sem("scores_ready"), sem("max_done"), sem("nmax_ready")
        misc_ready = sem("misc_ready")
        misc_freed = [sem("misc_freed0"), sem("misc_freed1")]
        shift_loaded = [sem(f"shift_loaded{g}") for g in range(NG)]
        scoresT_ready, exp_done, causal_done, pv_done = (sem(n) for n in ("scoresT_ready", "exp_done", "causal_done", "pv_done"))
        heads_drained = sem("heads_drained")
        var_ready, rstd_ready, x1_ready, x1b_ready, x2_ready, x2b_ready, x3_ready = (
            sem(n) for n in ("var_ready", "rstd_ready", "x1_ready", "x1b_ready", "x2_ready", "x2b_ready", "x3_ready"))
        split_hi = sem("split_hi")
        hidden_done = sem("hidden_done")
        spread_q, spread_k = [sem(f"spread_q{b}") for b in range(B)], [sem(f"spread_k{b}") for b in range(B)]
        stored = [sem(f"stored{b}") for b in range(B)]

        misc_no = {s: n for n, s in enumerate(s for s in plan if s[0] in MISC)}
        max_no = {s: n for n, s in enumerate(s for s in plan if s[0] == "max")}
        exp_no = {s: n for n, s in enumerate(s for s in plan if s[0] == "exp")}
        pv_no = {s: n for n, s in enumerate(s for s in plan if s[0] == "pv")}
        ln_no = {s: n for n, s in enumerate(s for s in plan if s[0] in NORMS)}
        causal_no = {s: n for n, s in enumerate(s for s in plan if s[0] == "pv" and kind(s[1]) == 2 and diagonal(s[1], s[2]) is not None)}
        hi_no = {s: n for n, s in enumerate(s for s in plan if s[0] == "proj" and s[2] in "qk")}

        def nth(s):
            return before(s, s[0])

        def last_exp(t, kt):
            return 1 + max(exp_no[("exp", t, j)] for j, bk in enumerate(exp_banks(t)) if bk[0] == kt)

        def unit_pvs(u):
            return 1 + max(n for p, n in pv_no.items() if p[1] // NG == u)

        def misc(s):
            n = misc_no[s]
            return mbank[n % MBANKS], misc_freed[n % MBANKS], n // MBANKS

        fold_chain = ["WqT", "Wq", "KET", "VE", "Wk", "Wv"]
        pro = PROLOGUE
        late = [s[1:] for s in plan if s[0] == "late"]
        split_jobs = [s for s in pro + late if s[0] in ("q1", "k1", "m")]
        pro_cols = {s: CHUNKS[s[1]][1] if s[0] in ("q1", "k1") else 512 for s in split_jobs}
        pro_bank = {s: i % (SBANKS + TBANKS) for i, s in enumerate(pro)}
        pro_use = {s: i // (SBANKS + TBANKS) for i, s in enumerate(pro)}
        PRO_LAST = [sum(1 for s in pro if pro_bank[s] == i) for i in range(SBANKS + TBANKS)]

        def drained(s):
            if s in pro:
                return pro_done[pro_bank[s]], pro_use[s] + 1
            _, freed, use = misc(("late",) + s)
            return freed, use + 1

        block = ctx.enter_context(nc.Block())

        def put(queue, scratch, halves, slots, signal):
            both, again = slots
            queue.dma_start(scratch[:, both:both + 2, :], halves).then_inc(signal, 16)
            queue.dma_start(scratch[:, again, :], halves[:, 0, :]).then_inc(signal, 16)

        def take_keys(queue, dst, scratch, signal):
            queue.dma_start(dst.bitcast(F32), scratch.rearrange("(g r) s t -> (r s) g t", g=NG)).then_inc(signal, 16)

        def take_queries(queue, u, scratch, t0, signal):
            dst = qm[:, u % QBUFS, :, :].rearrange("p (g j) t -> p g j t", g=NG)
            src = scratch.rearrange("(g j d) s t -> j (d s) g t", g=NG, j=HG)
            rows = SLOTS * HS
            for j in range(HG):
                queue.dma_start(dst[j * rows:(j + 1) * rows, :, j, :].bitcast(F32),
                             src[j, :, :, t0:t0 + T]).then_inc(signal, 16)

        def put_prologue(queue, n):
            name, c = s = split_jobs[n]
            done, value = drained(s)
            queue.wait_ge(done, value)
            cols = pro_cols[s]
            if name == "m":
                put(queue, scr_m[c], split0[n], K_SLOTS, spread0[n])
            else:
                t0 = CHUNKS[c][0]
                scratch, slots = (scr_q1, Q_SLOTS) if name == "q1" else (scr_k1, K_SLOTS)
                put(queue, scratch[:, :, t0:t0 + cols], split0[n][:, :, 0:cols], slots, spread0[n])

        def load_prologue(queue, n):
            name, c = split_jobs[n]
            queue.wait_ge(spread0[n], 16 * PUTS)
            if name == "k1":
                t0, cols = CHUNKS[c]
                take_keys(queue, ks1[0:STACK, :, t0:t0 + cols], scr_k1[:, :, t0:t0 + cols], k1_stacked[c])
            elif name == "m":
                if c < 2:
                    take_keys(queue, ks2[0:STACK, c, :, 0:MEM], scr_m[c], mem_stacked[c])
            else:
                queue.wait_ge(q_zeroed[c], 1)
                take_queries(queue, c, scr_q1, c * T, q_stacked[c])

        @block.sync
        def _(sp):
            sp.dma_start(w64_sb[:, :], w64).then_inc(w64_in, 16)
            sp.dma_start(wa_sb[:, :], wa).then_inc(wa_in, 16)
            sp.dma_start(xT_sb[:, 0:512], xT[:, 0:512]).then_inc(xT_in, 16)
            sp.dma_start(xT_sb[:, 512:], xT[:, 512:]).then_inc(xT_rest_in, 16)

            put_prologue(sp, 0)
            put_prologue(sp, 1)
            load_prologue(sp, 0)
            load_prologue(sp, 1)
            put_prologue(sp, 2)
            put_prologue(sp, 3)
            load_prologue(sp, 3)
            load_prologue(sp, 2)

            for s in plan:
                if s[0] == "shift":
                    t = s[1]
                    g = t % NG
                    _, freed, use = misc(s)
                    sp.wait_ge(freed, use + 1)
                    for r in range(2):
                        row = qm[STACK + r:STACK + r + 1, (t // NG) % QBUFS, g * HG:(g + 1) * HG, :]
                        sp.dma_start(row.bitcast(F32), shift_rows[r * HG:(r + 1) * HG, t % 2, :].bitcast(F32)).then_inc(shift_loaded[g], 16)
                elif s[0] == "inputs":
                    sp.dma_start(x_sb[:, :, :], x_rows.rearrange("(n p) c -> p n c", p=P)).then_inc(x_in, 16)
                    sp.dma_start(bias_sb[:, :], biases.to_broadcast([P, 2 * C])).then_inc(bias_in, 16)
                    sp.dma_start(sel_f[:, :], sel).then_inc(sel_in, 16)
                elif s[0] == "spread":
                    b, what = s[1], s[2]
                    _, freed, use = misc(("proj", b, what))
                    sp.wait_ge(freed, use + 1)
                    if what == "q":
                        put(sp, scr_q2[b], split_q[:, :, :].bitcast(F32), Q_SLOTS, spread_q[b])
                    else:
                        put(sp, scr_k2[b], split_k[:, :, :].bitcast(F32), K_SLOTS, spread_k[b])
                elif s[0] == "load_q":
                    u = s[1]
                    sp.wait_ge(pv_done, unit_pvs(u - QBUFS))
                    if u < B:
                        sp.wait_ge(spread0[split_jobs.index(("q1", 2))], 16 * PUTS)
                        take_queries(sp, u, scr_q1, u * T, q_stacked[u])
                    else:
                        sp.wait_ge(spread_q[u - B], 16 * PUTS)
                        take_queries(sp, u, scr_q2[u - B], 0, q_stacked[u])
                elif s[0] == "load_mem":
                    b = s[1]
                    sp.wait_ge(pv_done, unit_pvs(B + b - 2))
                    sp.wait_ge(spread0[split_jobs.index(("m", b))], 16 * PUTS)
                    take_keys(sp, ks2[0:STACK, b % 2, :, 0:MEM], scr_m[b], mem_stacked[b])
                elif s[0] == "load_own":
                    b = s[1]
                    sp.wait_ge(spread_k[b], 16 * PUTS)
                    take_keys(sp, ks2[0:STACK, b % 2, :, MEM:], scr_k2[b], self_stacked[b])
                elif s[0] == "mlp_out":
                    b = s[1]
                    sp.wait_ge(x3_ready, nth(s))
                    sp.dma_start(out[b].rearrange("(n p) c -> p n c", p=P), x1[:, b, :, :]).then_inc(stored[b], 16)
            for b in range(B):
                sp.wait_ge(stored[b], 16)

        @block.gpsimd
        def _(pool):
            nc.gpsimd.memset(qm[:, 0, :, :].bitcast(F32), 0.0).then_inc(q_zeroed[0], 1)
            nc.gpsimd.memset(neg[:, :, :], 0.0).then_inc(neg_step, 1)
            nc.gpsimd.memset(negT[:, :, :], 0.0).then_inc(neg_step, 1)
            pool.wait_ge(neg_step, 2)
            nc.gpsimd.affine_select(out=negT[:, :, :], in_=negT[:, :, :], compare_op=ALU.is_ge, fill=NEG, base=0,
                                    pattern=[[0, HG], [1, P]], channel_multiplier=-1).then_inc(consts_ready, 1)
            nc.gpsimd.affine_select(out=neg[:, :, :], in_=neg[:, :, :], compare_op=ALU.is_ge, fill=NEG, base=0,
                                    pattern=[[0, HG], [-1, P]], channel_multiplier=1).then_inc(consts_ready, 1)
            nc.gpsimd.memset(v1[:, :, :, HS], 1.0).then_inc(consts_ready, 1)
            nc.gpsimd.memset(v2[:, :, :, :, HS], 1.0).then_inc(consts_ready, 1)
            nc.gpsimd.memset(minus_half[:, :], -0.5).then_inc(consts_ready, 1)
            nc.gpsimd.memset(qm[:, 1, :, :].bitcast(F32), 0.0).then_inc(q_zeroed[1], 1)
            nc.gpsimd.memset(qm[:, 2, :, :].bitcast(F32), 0.0).then_inc(q_zeroed[2], 1)
            pool.wait_ge(q_zeroed[1], 1)
            pool.wait_ge(consts_ready, 5)
            pool.wait_ge(q_zeroed[2], 1)
            nc.gpsimd.memset(ks1[STACK:ROWS, :, :].bitcast(F32), 1.0).then_inc(ones_ready, 1)
            nc.gpsimd.memset(ks2[STACK:ROWS, :, :, :].bitcast(F32), 1.0).then_inc(ones_ready, 1)
            pool.wait_ge(ones_ready, 2)
            steps = 0
            for s in plan:
                if s[0] == "put0":
                    put_prologue(pool, s[1])
                elif s[0] == "load0":
                    load_prologue(pool, s[1])
                elif s[0] == "pv" and s in causal_no:
                    t, kt = s[1], s[2]
                    d = diagonal(t, kt)
                    pool.wait_ge(exp_done, last_exp(t, kt))
                    tile = probs[:, pv_no[s] % PRING, :, d * P:(d + 1) * P]
                    nc.gpsimd.affine_select(out=tile, in_=tile, compare_op=ALU.is_ge, fill=0.0, base=0,
                                            pattern=[[0, HG], [1, P]], channel_multiplier=-1).then_inc(causal_done, 1)
                elif s in ln_no:
                    n = ln_no[s]
                    pool.wait_ge(var_ready, n + 1)
                    nc.gpsimd.tensor_scalar_add(vpe[:, :], moments[:, :, 1], EPS).then_inc(pool_step, 1)
                    steps += 1
                    pool.wait_ge(pool_step, steps)
                    nc.gpsimd.tensor_tensor(rstd[:, :], vpe[:, :], minus_half[:, :], ALU.pow).then_inc(rstd_ready, 1)
                    b = s[1]
                    if n == 0:
                        pool.wait_ge(bias_in, 16)
                    if s[0] == "ln1":
                        pool.wait_ge(x1_ready, b + 1)
                        for i in range(QT):
                            last = nc.gpsimd.tensor_add(x1b[:, b, i, :], x1[:, b, i, :], bias_sb[:, 0:C])
                        last.then_inc(x1b_ready, 1)
                        if b == 0:
                            pool.wait_ge(sel_in, 16)
                            nc.gpsimd.tensor_copy(sel_r[:, :], sel_f[:, :]).then_inc(sel_ready, 1)
                    elif s[0] == "wo":
                        pool.wait_ge(x2_ready, b + 1)
                        for i in range(QT):
                            last = nc.gpsimd.tensor_add(x1b[:, b, i, :], x1[:, b, i, :], bias_sb[:, C:2 * C])
                        last.then_inc(x2b_ready, 1)

        @block.scalar
        def _(act):
            act.wait_ge(wa_in, 16)
            act.dma_start(wb_sb[:, :], wb).then_inc(wb_in, 16)
            act.dma_start(ctxT_sb[:, :], ctxT).then_inc(ctxT_in, 16)

            def drain_product(s, bk):
                if s[0] in ("v1", "vm"):
                    src = bk.rearrange("p (n h d) -> p n h d", n=4, h=NH)
                    dst = (v1[:, 4 * s[1]:4 * s[1] + 4] if s[0] == "v1" else v2[:, s[1], 0:4])[:, :, :, 0:HS]
                    for k in range(4):
                        last = nc.scalar.activation(dst[:, k], src[:, k], ACT.Copy)
                    last.then_inc(drained(s)[0], 1)
                else:
                    n = split_jobs.index(s)
                    cols = pro_cols[s]
                    nc.scalar.activation(split0[n][:, 0, 0:cols].bitcast(F32R), bk[:, 0:cols], ACT.Copy).then_inc(pro_hi, 1)

            for i, s in enumerate(pro):
                act.wait_ge(pro_ready, i + 1)
                drain_product(s, bank(pro_bank[s]))

            for s in plan:
                what = s[0]
                if what == "late":
                    act.wait_ge(misc_ready, misc_no[s] + 1)
                    drain_product(s[1:], misc(s)[0])
                elif what == "exp":
                    t, j = s[1], s[2]
                    n = exp_no[s]
                    kt, h, nh, q0 = exp_banks(t)[j]
                    ring = pv_no[("pv", t, kt)]
                    act.wait_ge(scoresT_ready, n + 1)
                    if h == 0 and ring >= PRING:
                        act.wait_ge(pv_done, ring - PRING + 1)
                    if h == 0 and ring < PRING:
                        act.wait_ge(spread0[ring], 16 * PUTS)
                    src = tbank[n % TBANKS].rearrange("p (h q) -> p h q", h=nh)
                    nc.scalar.activation(probs[:, ring % PRING, h:h + nh, q0:T], src, ACT.Exp,
                                         scale=SCALE).then_inc(exp_done, 1)
                elif what == "shift":
                    t = s[1]
                    g, u = t % NG, t // NG
                    m, freed, use = misc(s)
                    act.wait_ge(misc_ready, misc_no[s] + 1)
                    if t >= 2:
                        act.wait_ge(shift_loaded[(t - 2) % NG], 32 * ((t - 2) // NG + 1))
                    nc.scalar.activation(shift_rows[:, t % 2, :], m[0:2 * HG, 0:T], ACT.Copy).then_inc(freed, 1)
                elif what == "drain":
                    t = s[1]
                    act.wait_ge(pv_done, before(s, "pv"))
                    if t >= 2:
                        act.wait_ge(misc_ready, misc_no[("norm", t - 2)] + 1)
                    nc.scalar.activation(headsT[:, t % 2, :], obank[t % OBANKS][:, 0:T], ACT.Copy).then_inc(heads_drained, 1)
                elif what in ("x1T", "yT", "x2T"):
                    b = s[1]
                    m, freed, use = misc(s)
                    act.wait_ge(misc_ready, misc_no[s] + 1)
                    dst = {"x1T": x1T[:, b % 2, :], "yT": yT, "x2T": x2T[b]}[what]
                    nc.scalar.activation(dst, m[:, 0:T], ACT.Copy).then_inc(freed, 1)
                elif what == "proj":
                    b, w = s[1], s[2]
                    m, freed, use = misc(s)
                    act.wait_ge(misc_ready, misc_no[s] + 1)
                    if w == "v":
                        for k in range(QT):
                            last = nc.scalar.activation(v2[:, b, MEM // P + k, :, 0:HS],
                                                        m[:, k * P:(k + 1) * P].rearrange("p (h d) -> p h d", h=NH), ACT.Copy)
                        last.then_inc(freed, 1)
                    else:
                        if b:
                            act.wait_ge((spread_q if w == "q" else spread_k)[b - 1], 16 * PUTS)
                        dst = (split_q if w == "q" else split_k)[:, 0, :]
                        nc.scalar.activation(dst, m[:, 0:T], ACT.Copy).then_inc(split_hi, 1)
                elif what == "hidden" and s in hidden_on_act:
                    b, i = s[1], s[2]
                    m, freed, use = misc(s)
                    act.wait_ge(misc_ready, misc_no[s] + 1)
                    if b == B - 1:
                        act.wait_ge(misc_ready, misc_no[("mlp_mid", 0)] + 1)
                    for k in range(2):
                        f = 2 * i + k
                        last = nc.scalar.activation(hid[b][f], m[:, k * T:(k + 1) * T], ACT.Relu,
                                                    scale=wb_sb[:, WB["w1"] + f:WB["w1"] + f + 1],
                                                    bias=wb_sb[:, WB["b1"] + f:WB["b1"] + f + 1])
                    last.then_inc(freed, 1)

        @block.vector
        def _(dve):
            steps = [0]

            def link(ins):
                steps[0] += 1
                ins.then_inc(vec_step, 1)
                dve.wait_ge(vec_step, steps[0])

            for i in range(OBANKS):
                last = nc.vector.memset(obank[i][:, 0:T], 0.0)
            last.then_inc(vec_consts, 1)
            fold_dst = {"Wq": w1[:, 0, :], "WqT": fold[:, 0, :], "KET": fold[0:KVL, 1, :], "VE": fold[0:KVL, 2, :],
                        "Wv": w1[:, 2, :], "Wk": w1[:, 1, :]}
            for n, name in enumerate(fold_chain):
                dve.wait_ge(folded, n + 1)
                rows = KVL if name in ("KET", "VE") else P
                nc.vector.tensor_copy(fold_dst[name], fold_bank[n % 2][0:rows, 0:P]).then_inc(pro_done[6 + n % 2], 1)

            def low_half(s, bk):
                n, cols = split_jobs.index(s), pro_cols[s]
                dve.wait_ge(pro_hi, n + 1)
                nc.vector.tensor_sub(split0[n][:, 1, 0:cols].bitcast(F32R), bk[:, 0:cols],
                                     split0[n][:, 0, 0:cols]).then_inc(drained(s)[0], 1)

            for s in pro:
                if s in split_jobs:
                    low_half(s, bank(pro_bank[s]))
                elif s == ("v1", 0):
                    dve.wait_ge(wa_in, 16)
                    nc.vector.tensor_copy(ident_b[:, :], wa_sb[:, WA["ident"]:WA["ident"] + P]).then_inc(vec_consts, 1)
                    dve.wait_ge(wb_in, 16)
                    for f in range(FG):
                        last = nc.vector.tensor_scalar(w2x[:, f, :], wb_sb[:, WB["place"] + 32 * f:WB["place"] + 32 * f + 32],
                                                       wb_sb[:, WB["w2"] + f:WB["w2"] + f + 1], None, ALU.mult)
                    last.then_inc(vec_consts, 1)
                    nc.vector.memset(low_rows[0:FM, :], 0.0)
                    nc.vector.memset(low_rows[FM:P, :], -1.0).then_inc(vec_consts, 1)
            norm_stages = [s for s in plan if s[0] in NORMS]

            def res_free(s):
                if ln_no[s]:
                    last = norm_stages[ln_no[s] - 1]
                    dve.wait_ge({"ln1": x1_ready, "wo": x2_ready, "mlp_out": x3_ready}[last[0]], nth(last))

            def row_moments():
                for i in range(QT):
                    last = nc.vector.bn_stats(stats[:, i, :], res[:, i, :])
                link(last)
                for i in range(QT):
                    last = nc.vector.bn_aggr(moments[:, i, :], stats[:, i, :])
                last.then_inc(var_ready, 1)

            def normalise(s, dst):
                dve.wait_ge(rstd_ready, ln_no[s] + 1)
                for i in range(QT):
                    last = nc.vector.tensor_scalar(dst[:, i, :], res[:, i, :], moments[:, i, 0:1], rstd[:, i:i + 1],
                                                   ALU.subtract, ALU.mult)
                return last

            for s in plan:
                what = s[0]
                if what == "late":
                    if s[1:] in split_jobs:
                        low_half(s[1:], misc(s)[0])
                elif what == "max":
                    t, i = s[1], s[2]
                    n = max_no[s]
                    src, j, nh, qt = max_banks(t)[i]
                    dve.wait_ge(scores_ready, n + 1)
                    part = {"mem": 0, "own": 1}[src]
                    width = BANK // nh
                    tile = sbank[n % SBANKS].rearrange("p (h k) -> p h k", h=nh)
                    col = qt * HG + j
                    if kind(t) == 1:
                        nc.vector.tensor_reduce(nmax[:, t % 2, col:col + nh], tile, axis=AX.X, op=ALU.max,
                                                negate=True).then_inc(max_done, 1)
                    else:
                        nc.vector.tensor_reduce(pmax[:, t % 2, col:col + nh, part], tile, axis=AX.X,
                                                op=ALU.max).then_inc(max_done, 1)
                    if i == len(max_banks(t)) - 1:
                        dve.wait_ge(max_done, n + 1)
                        if kind(t) == 2:
                            link(nc.vector.tensor_reduce(nmax[:, t % 2, :], pmax[:, t % 2, :, :], axis=AX.X, op=ALU.max,
                                                         negate=True))
                        whole = nmax[:, t % 2, :].rearrange("p (q j) -> p q j", q=QT)
                        if t >= 2:
                            dve.wait_ge(misc_ready, misc_no[("shift", t - 2)] + 1)
                        high, low = nmax_s[:, t % 2, :, 0:HG], nmax_s[:, t % 2, :, HG:]
                        link(nc.vector.tensor_copy(high.bitcast(F32R), whole))
                        nc.vector.tensor_sub(low, whole, high).then_inc(nmax_ready, 1)
                elif what == "norm":
                    t = s[1]
                    g, u = t % NG, t // NG
                    m, freed, use = misc(s)
                    dve.wait_ge(misc_ready, misc_no[s] + 1)
                    o = m[:, 0:QT * HG * (HS + 1)].rearrange("p (n r) -> p n r", r=HS + 1)
                    link(nc.vector.reciprocal(rsum[:, t % 2, :], o[:, :, HS]))
                    sums = rsum[:, t % 2, :].rearrange("p (i j) -> p i j", i=QT).unsqueeze(3).to_broadcast([P, QT, HG, HS])
                    heads = o[:, :, 0:HS].rearrange("p (i j) d -> p i j d", i=QT)
                    dst = y[:, u % 2, :, g * HG * HS:(g + 1) * HG * HS].rearrange("p i (j d) -> p i j d", j=HG)
                    nc.vector.tensor_tensor(dst, heads, sums, ALU.mult).then_inc(freed, 1)
                elif what == "ln1":
                    b = s[1]
                    _, freed, use = misc(("norm", 4 * b + 3))
                    dve.wait_ge(freed, use + 1)
                    if b == 0:
                        dve.wait_ge(x_in, 16)
                        for n in range(PRING, SPLIT_JOBS):
                            dve.wait_ge(spread0[n], 16 * PUTS)
                    res_free(s)
                    link(nc.vector.tensor_add(res[:, :, :], y[:, b % 2, :, :], x_sb[:, QT * b:QT * (b + 1), :]))
                    row_moments()
                elif what == "apply" and s[1] == "ln1":
                    b = s[2]
                    normalise(s[1:], x1[:, b]).then_inc(x1_ready, 1)
                elif what == "proj" and s[2] in "qk":
                    b, w = s[1], s[2]
                    m, freed, use = misc(s)
                    dve.wait_ge(split_hi, hi_no[s] + 1)
                    sp_ = split_q if w == "q" else split_k
                    nc.vector.tensor_sub(sp_[:, 1, :], m[:, 0:T], sp_[:, 0, :].bitcast(F32)).then_inc(freed, 1)
                elif what == "wo":
                    b = s[1]
                    m, freed, use = misc(s)
                    dve.wait_ge(misc_ready, misc_no[s] + 1)
                    dve.wait_ge(x1b_ready, b + 1)
                    res_free(s)
                    nc.vector.tensor_add(res[:, :, :].rearrange("p n c -> p (n c)"), m[:, 0:QT * C],
                                         x1b[:, b, :, :].rearrange("p n c -> p (n c)")).then_inc(freed, 1)
                    dve.wait_ge(freed, use + 1)
                    row_moments()
                elif what == "apply" and s[1] == "wo":
                    b = s[2]
                    normalise(s[1:], x1[:, b]).then_inc(x2_ready, 1)
                elif what == "mlp_in":
                    b = s[1]
                    m, freed, use = misc(s)
                    dve.wait_ge(misc_ready, misc_no[s] + 1)
                    if nth(s) > 1:
                        dve.wait_ge(hidden_done, nth(s) - 1)
                    nc.vector.tensor_scalar(feat, m[:, 0:T], wb_sb[:, WB["bin"]:WB["bin"] + 1], None,
                                            ALU.add).then_inc(freed, 1)
                    dve.wait_ge(freed, use + 1)
                    link(nc.vector.tensor_copy(feat_h.bitcast(F32R), feat))
                    nc.vector.scalar_tensor_tensor(feat_s[b], feat_h, low_rows[:, 0:1], feat,
                                                   ALU.mult, ALU.add).then_inc(hidden_done, 1)
                elif what == "hidden" and s not in hidden_on_act:
                    b, i = s[1], s[2]
                    m, freed, use = misc(s)
                    dve.wait_ge(misc_ready, misc_no[s] + 1)
                    if b == B - 1:
                        dve.wait_ge(misc_ready, misc_no[("mlp_mid", 0)] + 1)
                    for k in range(2):
                        f = 2 * i + k
                        last = nc.vector.tensor_scalar(hid[b][f], m[:, k * T:(k + 1) * T],
                                                       wb_sb[:, WB["w1"] + f:WB["w1"] + f + 1],
                                                       wb_sb[:, WB["b1"] + f:WB["b1"] + f + 1], ALU.mult, ALU.add)
                    link(last)
                    for f in (2 * i, 2 * i + 1):
                        last = nc.vector.tensor_scalar(hid[b][f], hid[b][f], 0.0, None, ALU.max)
                    last.then_inc(freed, 1)
                elif what == "mlp_mid":
                    b = s[1]
                    m, freed, use = misc(s)
                    dve.wait_ge(misc_ready, misc_no[s] + 1)
                    nc.vector.tensor_scalar(midT[b], m[:, 0:T], wb_sb[:, WB["b2"]:WB["b2"] + 1], None,
                                            ALU.add).then_inc(freed, 1)
                elif what == "mlp_out":
                    b = s[1]
                    m, freed, use = misc(s)
                    dve.wait_ge(misc_ready, misc_no[s] + 1)
                    dve.wait_ge(x2b_ready, b + 1)
                    res_free(s)
                    nc.vector.tensor_add(res[:, :, :].rearrange("p n c -> p (n c)"), m[:, 0:QT * C],
                                         x1b[:, b, :, :].rearrange("p n c -> p (n c)")).then_inc(freed, 1)
                    dve.wait_ge(freed, use + 1)
                    row_moments()
                elif what == "apply":
                    b = s[2]
                    normalise(s[1:], x1[:, b]).then_inc(x3_ready, 1)

        @block.tensor
        def _(pe):
            ident = wa_sb[:, WA["ident"]:WA["ident"] + P]
            used_rows = ident.rearrange("p (j r) -> p j r", j=HG)[:, :, 0:HS + 1]

            def w64c(name):
                return w64_sb[:, W64[name]:W64[name] + P]

            def wbc(name):
                return wb_sb[:, WB[name]:WB[name] + P]

            pe.wait_ge(w64_in, 16)
            pe.wait_ge(wa_in, 16)
            operands = {"Wq": (w64c("dq"), w64c("uqT")), "WqT": (w64c("uqT"), w64c("dq")),
                        "VE": (wa_sb[:, WA["uv"]:WA["uv"] + KVL], wa_sb[:, WA["oT"]:WA["oT"] + P]),
                        "KET": (wa_sb[:, WA["uk"]:WA["uk"] + KVL], fold[:, 0, :]),
                        "Wv": (w64c("dkv"), fold[0:KVL, 2, :]), "Wk": (w64c("dkv"), fold[0:KVL, 1, :])}
            for n, name in enumerate(fold_chain):
                lhs, rhs = operands[name]
                if n >= 2:
                    pe.wait_ge(pro_done[6 + n % 2], n // 2)
                rows = KVL if name in ("KET", "VE") else P
                nc.tensor.matmul(fold_bank[n % 2][0:rows, 0:P], lhs, rhs, start=True, stop=True).then_inc(folded, 1)

            def product(s, bk):
                name, c = s
                if name in ("q1", "k1"):
                    t0, cols = CHUNKS[c]
                    return nc.tensor.matmul(bk[:, 0:cols], w1[:, 0 if name == "q1" else 1, :], xT_sb[:, t0:t0 + cols],
                                            start=True, stop=True)
                if name == "m":
                    return nc.tensor.matmul(bk, wbc("k"), ctxT_sb[:, MEM * c:MEM * (c + 1)], start=True, stop=True)
                for k in range(4):
                    col = 512 * c + k * P
                    lhs = xT_sb[:, col:col + P] if name == "v1" else ctxT_sb[:, col:col + P]
                    last = nc.tensor.matmul(bk[:, k * P:(k + 1) * P], lhs, w1[:, 2, :] if name == "v1" else wbc("v"),
                                            start=True, stop=True)
                return last

            for i, s in enumerate(pro):
                if pro_use[s]:
                    pe.wait_ge(pro_done[pro_bank[s]], pro_use[s])
                if i == 0:
                    pe.wait_ge(xT_in, 16)
                    pe.wait_ge(pro_done[6 + fold_chain.index("Wq") % 2], fold_chain.index("Wq") // 2 + 1)
                if i == 1:
                    for k in range(2):
                        pe.wait_ge(pro_done[6 + k], 3)
                if s == ("q1", 2):
                    pe.wait_ge(xT_rest_in, 16)
                if s == ("m", 0):
                    pe.wait_ge(wb_in, 16)
                    pe.wait_ge(ctxT_in, 16)
                product(s, bank(pro_bank[s])).then_inc(pro_ready, 1)
            pe.wait_ge(consts_ready, 5)
            pe.wait_ge(vec_consts, 4)

            def open_misc(s):
                m, freed, use = misc(s)
                if use:
                    pe.wait_ge(freed, use)
                return m

            for s in plan:
                what = s[0]
                if what == "late":
                    product(s[1:], open_misc(s)).then_inc(misc_ready, 1)
                elif what == "max":
                    t, i = s[1], s[2]
                    n = max_no[s]
                    g, u = t % NG, t // NG
                    b = u % B
                    if n < SBANKS:
                        pe.wait_ge(pro_done[n], PRO_LAST[n])
                    src, j, nh, qt = max_banks(t)[i]
                    if i == 0 and g == 0:
                        pe.wait_ge(q_stacked[u], 16 * HG)
                        if u < B:
                            pe.wait_ge(k1_stacked[min(b, 2)], 16)
                        else:
                            pe.wait_ge(mem_stacked[b], 16)
                            pe.wait_ge(self_stacked[b], 16)
                    if n >= SBANKS:
                        pe.wait_ge(max_done, n - SBANKS + 1)
                    sk = sbank[n % SBANKS]
                    width = BANK // nh

                    def lhs(jj):
                        return qm[0:STACK, u % QBUFS, g * HG + jj, qt * P:(qt + 1) * P]

                    if src == "mem":
                        last = nc.tensor.matmul(sk, lhs(j), ks2[0:STACK, b % 2, g, 0:MEM], start=True, stop=True)
                    else:
                        for k in range(nh):
                            o = sk[:, k * width:(k + 1) * width]
                            if u < B:
                                keys = ks1[0:STACK, g, b * T:b * T + width]
                            else:
                                keys = ks2[0:STACK, b % 2, g, MEM:MEM + width]
                            nc.tensor.matmul(o, lhs(j + k), keys, start=(k == 0), stop=False)
                        tile = sk.rearrange("p (h k) -> p h k", h=nh)[:, :, width - P:width]
                        last = nc.tensor.matmul(tile, ident_b[:, :], neg[:, 0:nh, :], start=False, stop=True)
                    last.then_inc(scores_ready, 1)
                elif what == "shift":
                    t = s[1]
                    m = open_misc(s)
                    pe.wait_ge(nmax_ready, t + 1)
                    for qt in range(QT):
                        last = nc.tensor.transpose(m[0:2 * HG, qt * P:(qt + 1) * P], nmax_s[:, t % 2, qt, :], ident)
                    last.then_inc(misc_ready, 1)
                elif what == "exp":
                    t, j = s[1], s[2]
                    n = exp_no[s]
                    g, u = t % NG, t // NG
                    b = u % B
                    kt, h, nh, q0 = exp_banks(t)[j]
                    if j == 0 and g == 0:
                        pe.wait_ge(ones_ready, 1 if u < B else 2)
                    if j == 0:
                        pe.wait_ge(shift_loaded[g], 32 * (u + 1))
                    if n < TBANKS:
                        pe.wait_ge(pro_done[SBANKS + n], PRO_LAST[SBANKS + n])
                    else:
                        pe.wait_ge(exp_done, n - TBANKS + 1)
                    keys = (ks1[0:ROWS, g, b * T + kt * P:b * T + (kt + 1) * P] if u < B
                            else ks2[0:ROWS, b % 2, g, kt * P:(kt + 1) * P])
                    queries = qm[0:ROWS, u % QBUFS, g * HG + h:g * HG + h + nh, q0:T]
                    if kind(t) == 2 or diagonal(t, kt) is None:
                        nc.tensor.matmul(tbank[n % TBANKS], keys, queries, start=True, stop=True).then_inc(scoresT_ready, 1)
                    else:
                        nc.tensor.matmul(tbank[n % TBANKS], keys, queries, start=True, stop=False)
                        tile = tbank[n % TBANKS].rearrange("p (h q) -> p h q", h=nh)[:, :, 0:P]
                        nc.tensor.matmul(tile, ident_b[:, :], negT[:, 0:nh, :], start=False, stop=True).then_inc(scoresT_ready, 1)
                elif what == "pv":
                    t, kt = s[1], s[2]
                    g, u = t % NG, t // NG
                    b = u % B
                    last_kt = key_tiles(t) - 1
                    pe.wait_ge(exp_done, last_exp(t, kt))
                    if s in causal_no:
                        pe.wait_ge(causal_done, causal_no[s] + 1)
                    if kt == 0 and t >= OBANKS:
                        pe.wait_ge(heads_drained, t - OBANKS + 1)
                    q0 = P if kt == last_kt else 0
                    for j in range(HG):
                        v = (v1[:, b * QT + kt, g * HG + j, :] if u < B else v2[:, b, kt, g * HG + j, :])
                        last = nc.tensor.matmul(obank[t % OBANKS][32 * j:32 * j + HS + 1, q0:T], v,
                                                probs[:, pv_no[s] % PRING, j, q0:T], start=(kt == 0), stop=(kt == last_kt))
                    last.then_inc(pv_done, 1)
                elif what == "norm":
                    t = s[1]
                    m = open_misc(s)
                    pe.wait_ge(heads_drained, t + 1)
                    for qt in range(QT):
                        last = nc.tensor.matmul(m[:, qt * HG * (HS + 1):(qt + 1) * HG * (HS + 1)],
                                                headsT[:, t % 2, qt * P:(qt + 1) * P], used_rows, start=True, stop=True)
                    last.then_inc(misc_ready, 1)
                elif what in ("x1T", "yT", "x2T"):
                    b = s[1]
                    m = open_misc(s)
                    if what == "x1T":
                        pe.wait_ge(x1_ready, b + 1)
                        src = x1[:, b]
                    elif what == "yT":
                        _, freed, use = misc(("norm", NG * (B + b) + NG - 1))
                        pe.wait_ge(freed, use + 1)
                        src = y[:, (B + b) % 2]
                    else:
                        pe.wait_ge(x2_ready, b + 1)
                        src = x1[:, b]
                    for i in range(QT):
                        last = nc.tensor.transpose(m[:, i * P:(i + 1) * P], src[:, i, :], ident)
                    last.then_inc(misc_ready, 1)
                elif what == "proj":
                    b, w = s[1], s[2]
                    m = open_misc(s)
                    _, freed, use = misc(("x1T", b))
                    pe.wait_ge(freed, use + 1)
                    if w == "v":
                        for i in range(QT):
                            last = nc.tensor.matmul(m[:, i * P:(i + 1) * P], x1T[:, b % 2, i * P:(i + 1) * P], wbc("v"),
                                                    start=True, stop=True)
                    else:
                        last = nc.tensor.matmul(m[:, 0:T], wbc(w), x1T[:, b % 2, :], start=True, stop=True)
                    last.then_inc(misc_ready, 1)
                elif what == "wo":
                    m = open_misc(s)
                    _, freed, use = misc(("yT", s[1]))
                    pe.wait_ge(freed, use + 1)
                    for i in range(QT):
                        last = nc.tensor.matmul(m[:, i * P:(i + 1) * P], yT[:, i * P:(i + 1) * P], wbc("out"), start=True, stop=True)
                    last.then_inc(misc_ready, 1)
                elif what == "mlp_in":
                    m = open_misc(s)
                    _, freed, use = misc(("x2T", s[1]))
                    pe.wait_ge(freed, use + 1)
                    nc.tensor.matmul(m[:, 0:T], wbc("in2"), x2T[s[1]], start=True, stop=True).then_inc(misc_ready, 1)
                elif what == "hidden":
                    b, i = s[1], s[2]
                    m = open_misc(s)
                    pe.wait_ge(sel_ready, 1)
                    pe.wait_ge(hidden_done, nth(("mlp_in", b)))
                    for k in range(2):
                        f = 2 * i + k
                        last = nc.tensor.matmul(m[:, k * T:(k + 1) * T], sel_r[:, f * P:(f + 1) * P], feat_s[b], start=True, stop=True)
                    last.then_inc(misc_ready, 1)
                elif what == "mlp_mid":
                    m = open_misc(s)
                    for f in range(FG):
                        c = f % 4
                        if f % 2 == 0:
                            _, freed, use = misc(("hidden", s[1], f // 2))
                            pe.wait_ge(freed, use + 1)
                        last = nc.tensor.matmul(m[32 * c:32 * c + 32, 0:T], w2x[:, f, :], hid[s[1]][f],
                                                start=(f < 4), stop=(f >= 4))
                    last.then_inc(misc_ready, 1)
                elif what == "mlp_out":
                    m = open_misc(s)
                    _, freed, use = misc(("mlp_mid", s[1]))
                    pe.wait_ge(freed, use + 1)
                    for i in range(QT):
                        last = nc.tensor.matmul(m[:, i * P:(i + 1) * P], midT[s[1]][:, i * P:(i + 1) * P], wbc("fout"), start=True, stop=True)
                    last.then_inc(misc_ready, 1)


def _placed(a):
    import numpy as np
    o = np.zeros((P,) + a.shape[1:], a.dtype)
    for c in range(4):
        for k in range(2):
            o[32 * c + 8 * k:32 * c + 8 * k + 8] = a[8 * c + 32 * k:8 * c + 32 * k + 8]
    return o


def kernel(**inputs):
    import numpy as np
    import concourse.bacc as bacc
    from concourse.bass_utils import run_bass_kernel_spmd

    a = {k.replace("L0_", ""): np.asarray(v) for k, v in inputs.items()}
    f32 = np.float32
    hidden = np.arange(FM * FH).reshape(FG, P)
    feature = hidden // FH
    sel = (np.arange(P)[:, None, None] % FM == feature[None]).reshape(P, FG * P).astype(f32)
    col = (np.arange(FG)[:, None] // 4) * 8 + (np.arange(P)[None, :] // FH)
    place = (np.arange(32)[None, None, :] == col.T[:, :, None]).reshape(P, FG * 32).astype(f32)

    x, c = a["x"], a["ctx_1024"]
    cols = lambda w: w.reshape(FG, P).T
    arrays = {
        "x_rows": x.reshape(B * T, C),
        "xT": x.reshape(B * T, C).T,
        "ctxT": c.reshape(B * MEM, C).T,
        "w64": np.concatenate([a["attn_W_dq"], a["attn_W_uq"].T, a["attn_W_dkv"]], 1),
        "wa": np.concatenate([a["attn_W_uk"], a["attn_W_uv"], a["attn_W_o"].T, np.eye(P, dtype=f32)], 1),
        "wb": np.concatenate([a["xattn_Wq"], a["xattn_Wkv"], a["xattn_Wout"], a["ffn_Win"], a["ffn_Win"],
                              _placed(a["ffn_Wout"]), np.concatenate([a["ffn_bin_"], a["ffn_bin_"]])[:, None],
                              cols(a["ffn_W1"]), cols(a["ffn_b1"]), cols(a["ffn_W2"]),
                              _placed(a["ffn_b2"][:, None]), place], 1),
        "sel": sel,
        "biases": np.concatenate([a["xattn_bout"], a["ffn_bout"]])[None, :],
    }
    arrays = {k: np.ascontiguousarray(v) for k, v in arrays.items()}
    nc = bacc.Bacc("TRN2", target_bir_lowering=False, num_devices=1)
    args = [nc.dram_tensor(k, v.shape, F32, kind="ExternalInput").ap() for k, v in arrays.items()]
    out = nc.dram_tensor("out", (B, T, C), F32, kind="ExternalOutput").ap()
    decoder_layer(nc, *args, out)
    r = run_bass_kernel_spmd(nc, [arrays], core_ids=[0])
    return r.results[0]["out"]
```
